# Optimizing a Trainium2 kernel written in Bass

```python
import numpy as np
import jax
import jax.numpy as jnp

def _softmax(x, axis=-1):
    return jax.nn.softmax(x, axis=axis)

def _gelu(x):
    return jax.nn.gelu(x, approximate=True)

def _silu(x):
    return jax.nn.silu(x)

def _sigmoid(x):
    return jax.nn.sigmoid(x)

def _layernorm(x, axis=-1, eps=1e-05):
    m = jnp.mean(x, axis=axis, keepdims=True)
    v = jnp.var(x, axis=axis, keepdims=True)
    return (x - m) / jnp.sqrt(v + eps)

def _scatter_add(tgt, idx, src, axis=0):
    return tgt.at[idx].add(src)

def _segment_sum(src, seg, n):
    return jax.ops.segment_sum(src, seg, n)
kernel_name = 'mk_lm_tower_d1_tok_ids1024_r4_02018a'

def setup_inputs(seed: int=0):
    np.random.seed(seed)
    _w = jnp.asarray

    def _rec_inputs():
        import jax
        import jax.numpy as jnp
        _rk = jax.random.key(seed)
        x = jax.random.randint(jax.random.fold_in(_rk, 1), (2, 1024), 0, 12564, jnp.int32)
        return x
    x = _rec_inputs()

    def _L0_tok_setup():
        import jax, jax.numpy as jnp
        import numpy as np
        VOCAB = 50257
        D_MODEL = 256
        BATCH = 4
        SEQ = 1024
        key = jax.random.key(seed)
        k1, k2 = jax.random.split(key)
        x = jax.random.randint(k1, (BATCH, SEQ), 0, VOCAB, dtype=jnp.int64 if jax.config.jax_enable_x64 else jnp.int32)
        W = (jax.random.normal(k2, (VOCAB, D_MODEL), dtype=jnp.float32) * 0.02).clip(-0.04, 0.04)
        return {'x': x, 'W': W}
    _L0_tok_all = _L0_tok_setup()
    _L0_tok_in = {k: v for k, v in _L0_tok_all.items() if k in ('W',)}
    del _L0_tok_all

    def _L0_attn_setup():
        import jax, jax.numpy as jnp
        import numpy as np
        import math
        D_MODEL = 256
        NUM_HEADS = 16
        HEAD_DIM = D_MODEL // NUM_HEADS
        REPETITIONS = 3
        NEG = -10000.0

        def _self_attention(q, k, v, mask):
            scale = 1.0 / math.sqrt(q.shape[-1])
            scores = jnp.einsum('bthd,bshd->bhts', q, k * scale) + mask
            attn = jax.nn.softmax(scores, axis=-1)
            return jnp.einsum('bhts,bshd->bthd', attn, v)
        key = jax.random.key(seed)
        ks = jax.random.split(key, 5)
        B, S = (2, 512)
        x = jax.random.normal(ks[0], (B, S, D_MODEL), dtype=jnp.float32)
        Wqkv_w = jax.random.normal(ks[1], (3 * D_MODEL, D_MODEL), dtype=jnp.float32) * (1.0 / math.sqrt(D_MODEL))
        Wqkv_b = jax.random.normal(ks[2], (3 * D_MODEL,), dtype=jnp.float32) * 0.02
        out_w = jax.random.normal(ks[3], (D_MODEL, D_MODEL), dtype=jnp.float32) * (1.0 / math.sqrt(D_MODEL))
        out_b = jax.random.normal(ks[4], (D_MODEL,), dtype=jnp.float32) * 0.02
        return {'x': x, 'Wqkv_w': Wqkv_w, 'Wqkv_b': Wqkv_b, 'out_w': out_w, 'out_b': out_b}
    _L0_attn_all = _L0_attn_setup()
    _L0_attn_in = {k: v for k, v in _L0_attn_all.items() if k in ('Wqkv_w', 'Wqkv_b', 'out_w', 'out_b')}
    del _L0_attn_all

    def _L0_ffn_setup():
        import jax, jax.numpy as jnp
        import numpy as np
        A, M, H = (4, 256, 256)
        E, N = (8, 1024)
        key = jax.random.key(seed)
        kx, k1, k2 = jax.random.split(key, 3)
        x = jax.random.normal(kx, (A, M, H), dtype=jnp.float32)
        w1 = jax.random.normal(k1, (E, H, N), dtype=jnp.float32) * 0.02
        w2 = jax.random.normal(k2, (E, N, H), dtype=jnp.float32) * 0.02
        return {'x': x, 'w1': w1, 'w2': w2}
    _L0_ffn_all = _L0_ffn_setup()
    _L0_ffn_in = {k: v for k, v in _L0_ffn_all.items() if k in ('w1', 'w2')}
    del _L0_ffn_all
    return {'x': x, 'L0_tok_W': _L0_tok_in['W'], 'L0_attn_Wqkv_w': _L0_attn_in['Wqkv_w'], 'L0_attn_Wqkv_b': _L0_attn_in['Wqkv_b'], 'L0_attn_out_w': _L0_attn_in['out_w'], 'L0_attn_out_b': _L0_attn_in['out_b'], 'L0_ffn_w1': _L0_ffn_in['w1'], 'L0_ffn_w2': _L0_ffn_in['w2']}

def reference(x, L0_tok_W, L0_attn_Wqkv_w, L0_attn_Wqkv_b, L0_attn_out_w, L0_attn_out_b, L0_ffn_w1, L0_ffn_w2):
    import jax
    import jax.numpy as jnp

    def _L0_tok_ref(x, W):
        import jax, jax.numpy as jnp
        import numpy as np
        VOCAB = 50257
        D_MODEL = 256
        BATCH = 4
        SEQ = 1024
        return jnp.take(W, x, axis=0)

    def _L0_attn_ref(x, Wqkv_w, Wqkv_b, out_w, out_b):
        import jax, jax.numpy as jnp
        import numpy as np
        import math
        D_MODEL = 256
        NUM_HEADS = 16
        HEAD_DIM = D_MODEL // NUM_HEADS
        REPETITIONS = 3
        NEG = -10000.0

        def _self_attention(q, k, v, mask):
            scale = 1.0 / math.sqrt(q.shape[-1])
            scores = jnp.einsum('bthd,bshd->bhts', q, k * scale) + mask
            attn = jax.nn.softmax(scores, axis=-1)
            return jnp.einsum('bhts,bshd->bthd', attn, v)
        B, S, _ = x.shape
        qkv = x @ Wqkv_w.T + Wqkv_b
        qkv = qkv.reshape(B, S, 3, NUM_HEADS, HEAD_DIM)
        q, k, v = (qkv[:, :, 0], qkv[:, :, 1], qkv[:, :, 2])
        mask = jnp.triu(jnp.full((S, S), NEG, dtype=x.dtype), 1)
        context = _self_attention(q, k, v, mask)
        for _ in range(REPETITIONS - 1):
            context = _self_attention(context, k, v, mask)
        out = context.reshape(B, S, D_MODEL) @ out_w.T + out_b
        return out

    def _L0_ffn_ref(x, w1, w2):
        import jax, jax.numpy as jnp
        import numpy as np
        A, M, H = (4, 256, 256)
        E, N = (8, 1024)
        mid = jnp.einsum('amh,ehn->aemn', x, w1)
        out = jnp.einsum('aemn,enh->amh', mid, w2)
        return out
    h = _L0_tok_ref(x, L0_tok_W)
    h = h + _L0_attn_ref(_layernorm(h, axis=-1), L0_attn_Wqkv_w, L0_attn_Wqkv_b, L0_attn_out_w, L0_attn_out_b)
    h = h + _L0_ffn_ref(_layernorm(h, axis=-1), L0_ffn_w1, L0_ffn_w2)
    return h

_drawn_inputs = setup_inputs


def setup_inputs(seed=0):
    import zlib

    import numpy as np

    out = dict(_drawn_inputs(seed))
    spreads = {}
    factors = {}
    for name, (base, spread) in spreads.items():
        noise = np.random.default_rng([zlib.crc32(name.encode()), seed]).standard_normal(out[name].shape)
        drawn = base * np.exp(spread * noise) if base else spread * noise
        out[name] = jnp.asarray(drawn.astype(out[name].dtype))
    for name, factor in factors.items():
        out[name] = (out[name] * factor).astype(out[name].dtype)
    return out
```

```python
from contextlib import ExitStack

import concourse.bass as bass
from concourse import mybir

ACT = mybir.ActivationFunctionType
ALU = mybir.AluOpType
AX = mybir.AxisListType
F32 = mybir.dt.float32
BF16 = mybir.dt.bfloat16
I32 = mybir.dt.int32

P = 128
B = 2
S = 1024
D = 256
HD = 16
NEXP, N_FF = 8, 1024
ROUNDS = 3
HG = 4
GROUPS = D // (HD * HG)
GW = HD * HG
BG = B * GROUPS
STEPS = ROUNDS * BG
TB = S // P
NT = B * TB
KS = 96
KM = 99
EPS = 1e-5
KEY_SCALE = HD ** -0.5
NEG = -10000.0
ROW_LOW = -3.0e38

NAT = []
for _i in range(TB):
    for _c in range(1 if _i < 4 else 2):
        _w = P * (_i + 1) if _i < 4 else (512 if _c == 0 else P * (_i - 3))
        _nh = 4 if _w == 128 else 2 if _w == 256 else 1
        for _h in range(0, HG, _nh):
            NAT.append((_i, _c, list(range(_h, _h + _nh)), 512 * _c, _w, _i < 4 or _c == 1))
NN = len(NAT)

QUADS = []
for _t in range(2):
    for _j in range(4 * (_t + 1)):
        _k = max(0, _j - 4 * _t)
        QUADS.append((_t, _j, 512 - P * _k, P * _k, _j >= 4 * _t))
NQ = len(QUADS)


def head_chunks(w):
    return ([[0, 1], [2, 3]], 512) if w > 256 else ([[0, 1, 2, 3]], w)


CHUNKS_TO = [0]
MASKS_TO = [0]
for _q in QUADS:
    CHUNKS_TO.append(CHUNKS_TO[-1] + len(head_chunks(_q[2])[0]))
    MASKS_TO.append(MASKS_TO[-1] + len(head_chunks(_q[2])[0]) * _q[4])
NC, NM = CHUNKS_TO[-1], MASKS_TO[-1]

NAT_QUADS = 9
NAT_AT = [[] for _ in range(NQ)]
_cols = [sum(q[2] for q in QUADS[:k + 1]) for k in range(NAT_QUADS)]
_at, _done, _all = 0, 0, sum(len(c[2]) * c[4] for c in NAT)
for _n, _c in enumerate(NAT):
    _done += len(_c[2]) * _c[4]
    while _at < NAT_QUADS - 1 and _done * _cols[-1] > _cols[_at] * _all:
        _at += 1
    NAT_AT[_at].append(_n)

CTX_QUAD = (3, 5)
SPLIT_QUAD = 6
QT_QUAD = (8, 10)
MAX_QUAD = 10
EVAC1_QUAD, EVAC0_QUAD = 1, 5

PIECES_Q = (0, 1, 2, 0, 1, 0)
PIECES_K = (0, 0, 0, 1, 1, 2)
LOADS = len(PIECES_Q) + len(PIECES_K) + 1
CWRITES = 4
PROJ_WRITES = 48
WBASE = PROJ_WRITES // 3 * 16


def wait_alone(eng, sem, value, tally):
    eng.wait_ge(sem, value)
    eng.sem_inc(tally, 1)


class Step:

    def __init__(self, i, off):
        self.i, self.off = i, off
        self.n = 3 * i + off
        self.u = off % 3
        self.q = i + off // 3

    def add(self, d):
        return Step(self.i, self.off + d)


def over_steps(eng, step):
    step(Step(0, 0), has_ctx=False, has_next=True, has_load=True)
    turns = (STEPS - 3) // 3
    with eng.Fori(0, turns) as i:
        for k in range(3):
            step(Step(i, 1 + k), has_ctx=True, has_next=True, has_load=True)
    step(Step(turns, 1), has_ctx=True, has_next=True, has_load=False)
    step(Step(turns, 2), has_ctx=True, has_next=False, has_load=False)


def layer(nc, x, tok_w, wqkv, bqkv, out_w, out_b, w1, w2, out):
    with ExitStack() as ctx:
        def sb(name, shape, dt):
            return ctx.enter_context(nc.sbuf_tensor(name, shape, dt))

        def sem(name):
            return ctx.enter_context(nc.semaphore(name))

        q_d = nc.dram_tensor("q_parts", [BG, 3, GW, S], BF16, kind="Internal").ap()
        k_d = nc.dram_tensor("k_parts", [BG, 3, GW, S], BF16, kind="Internal").ap()
        v_d = nc.dram_tensor("v_ones", [BG, P, TB, 2 * GW], F32, kind="Internal").ap()
        c_d = nc.dram_tensor("context", [BG, P, TB * GW], F32, kind="Internal").ap()

        ps = ctx.enter_context(nc.psum_tensor("ps", [P, 8, 512], F32))
        ST_BANK, NAT_BANK, PV_BANK, MISC_BANK = 0, 4, 6, 7
        misc = ps[:, MISC_BANK, :]
        misc_bf = misc.bitcast(BF16)

        h = sb("h", [P, NT, D], F32)
        xT = sb("xT", [P, 2, B * S], F32)
        wn = sb("wn", [P, 6, D], F32)
        wT = sb("wT", [P, 2, 3 * D], F32)
        own = sb("own", [P, 2, D], F32)
        owp = sb("owp", [P, 2, D], F32)
        woT = sb("woT", [P, 2, D], F32)
        bias_qk = sb("bias_qk", [P, 4], F32)
        bias_v = sb("bias_v", [P, D], F32)
        bias_o = sb("bias_o", [P, D], F32)
        idx_row = sb("idx_row", [NT, P], I32)
        idx_f = sb("idx_f", [NT, P], F32)
        idx = sb("idx", [P, NT], I32)
        bias_row = sb("bias_row", [4, P], F32)
        bias_p = sb("bias_p", [4, P], F32)
        identf = sb("identf", [P, P], F32)
        identb = sb("identb", [P, P], BF16)
        mask_l = sb("mask_l", [P, P], BF16)
        mask_r = sb("mask_r", [P, P], BF16)
        stats = sb("stats", [P, NT, 6], F32)
        mv = sb("mv", [P, NT, 2], F32)
        var = sb("var", [P, NT], F32)
        std = sb("std", [P, NT], F32)
        rstd = sb("rstd", [P, NT], F32)
        hn = sb("hn", [P, 4, D], F32)
        vt = sb("vt", [P, 2, GROUPS, HG, 2, HD], F32)
        w12 = sb("w12", [P, 2, D], F32)
        work = sb("work", [P, 10240], F32)
        qst = sb("qst", [P, 3, HG * S], BF16)
        kst = sb("kst", [P, 3, HG * S], BF16)
        vst = sb("vst", [P, 3, TB, HG, 2 * HD], F32)
        mx = sb("mx", [P, HG, TB, 2], F32)
        negm = sb("negm", [P, HG * TB], F32)
        mrest = sb("mrest", [P, HG * TB], F32)
        msp = sb("msp", [P, 3, HG * TB], BF16)
        mrow = sb("mrow", [P, P], BF16)
        cT = sb("cT", [P, 2, 512], F32)
        rden = sb("rden", [P, 16], F32)
        cn = sb("cn", [P, TB, HD, HG], F32)
        crest = sb("crest", [P, TB, GW], F32)
        qn = sb("qn", [P, TB, 3, GW], BF16)
        qT1 = sb("qT1", [P, S], BF16)
        qT2 = sb("qT2", [GW, S], BF16)

        w1b = work[:, 0:4096].rearrange("p (u k n) -> p u k n", u=2, k=2)
        w2b = work[:, 4096:8192].rearrange("p (u k n) -> p u k n", u=2, k=8)
        w1T = work[:, 8192:10240].rearrange("p (k n) -> p k n", k=8)
        prob = work[:, 0:6144].rearrange("p (s c) -> p s c", s=3)
        cx = work[:, 6144:10240].rearrange("p (k c) -> p k c", k=NT)
        hn2 = cx
        res = work[:, 1024:2048].rearrange("p (k n) -> p k n", k=4)
        xs = qst[:, 0, 0:3072].bitcast(F32).rearrange("p (r n) -> p r n", r=3)
        rs = qst[:, 1, 0:3072].bitcast(F32).rearrange("p (r n) -> p r n", r=3)
        parts = [t[:, 2, 1536 * r:1536 * (r + 1)].rearrange("p (a n) -> p a n", a=3)
                 for t in (qst, kst) for r in range(2)]

        in_x, in_w, in_b = sem("in_x"), sem("in_w"), sem("in_b")
        consts, ones_set = sem("consts"), sem("ones_set")
        rows_ready, rows_turned, idx_ready = sem("rows_ready"), sem("rows_turned"), sem("idx_ready")
        gathered = [sem(f"gathered{n}") for n in range(4)]
        dchain = sem("dve_chain")
        pchain = sem("pool_chain")
        var_ready, std_ready = sem("var_ready"), sem("std_ready")
        hn_ready = sem("hn_ready")
        owp_ready = sem("owp_ready")
        job_done, job_act, job_dve = sem("job_done"), sem("job_act"), sem("job_dve")
        x_hi, x_rest, x_mid, x_lo = sem("x_hi"), sem("x_rest"), sem("x_mid"), sem("x_lo")
        part_out = [sem(f"part_out{r}") for r in range(4)]
        vt_out = [sem(f"vt_out{r}") for r in range(2)]
        w_loaded = [sem(f"w_loaded{r}") for r in range(2)]
        w_turned, w_evac_act, w_evac_dve = sem("w_turned"), sem("w_evac_act"), sem("w_evac_dve")
        w_mul, w_acc = sem("w_mul"), sem("w_acc")
        stack_in = [sem(f"stack_in{u}") for u in range(3)]
        max_in = [sem(f"max_in{u}") for u in range(3)]
        scratch = [sem(f"scratch{u}") for u in range(3)]
        nat_ready, nat_used = sem("nat_ready"), sem("nat_used")
        max_chain, max_turned, max_rows = sem("max_chain"), sem("max_turned"), sem("max_rows")
        st_ready, exp_done, mask_done, prob_used = (sem("st_ready"), sem("exp_done"),
                                                    sem("mask_done"), sem("prob_used"))
        pv_copied = sem("pv_copied")
        ctx_turned, den_ready, ctx_ready = sem("ctx_turned"), sem("den_ready"), sem("ctx_ready")
        split_chain = sem("split_chain")
        q_turned, q_rows = sem("q_turned"), sem("q_rows")
        ctx_in = sem("ctx_in")
        h1_ready, fin_ready = sem("h1_ready"), sem("fin_ready")
        e_job, e_act, e_dve = sem("e_job"), sem("e_act"), sem("e_dve")
        e_var, e_std = sem("e_var"), sem("e_std")
        e_hn = sem("e_hn")
        pool_tally, pe_tally = sem("pool_tally"), sem("pe_tally")
        stored = [sem(f"stored{r}") for r in range(4)]

        jobs = [("wqkv", kc, half) for kc in range(2) for half in range(2)] + [("wo", 0, 0)]
        jobs += [("turn", 0, 0), ("turn", 1, 0)]
        for n in range(4):
            if n < 3:
                jobs += [("turn", 2 * n + 2, 0), ("turn", 2 * n + 3, 0)]
            jobs += [("qk", m, n) for m in range(4)]
            jobs += [("v", 2 * n, 0), ("v", 2 * n + 1, 0)]
        RING = 6
        by_dve = [j[0] in ("qk", "v") for j in jobs]

        def copied(e, k):
            if by_dve[k]:
                e.wait_ge(job_dve, sum(by_dve[:k + 1]))
            else:
                e.wait_ge(job_act, k + 1 - sum(by_dve[:k + 1]))

        block = ctx.enter_context(nc.Block())

        @block.sync
        def _(sp):
            sp.dma_start(idx_row[:], x.rearrange("b (k p) -> (b k) p", p=P)).then_inc(in_x, 16)
            sp.dma_start(bias_row[:], bqkv[0:2 * D].rearrange("(m p) -> m p", p=P)).then_inc(in_x, 16)
            for m in range(4):
                for g in range(2):
                    row = m * P + g * GW
                    sp.dma_start(wn[g * GW:(g + 1) * GW, m, :],
                                 wqkv[row:row + GW, :].rearrange("(h d) c -> d h c", h=HG)).then_inc(in_w, 16)
            sp.dma_start(wn[:, 4:6, :], wqkv[2 * D:3 * D, :].rearrange("(m p) c -> p m c", p=P)).then_inc(in_w, 16)
            sp.dma_start(own[:], out_w.rearrange("(m p) c -> p m c", p=P)).then_inc(in_w, 16)
            sp.dma_start(bias_v[:], bqkv[2 * D:3 * D].partition_broadcast(P)).then_inc(in_b, 16)
            sp.dma_start(bias_o[:], out_b.partition_broadcast(P)).then_inc(in_b, 16)

            writes = 0
            for n in range(4):
                b, half = n // 2, n % 2
                for m in range(4):
                    x_n = 4 * n + m
                    sp.wait_ge(x_lo, x_n + 1)
                    for g in range(2):
                        dst = (q_d if m < 2 else k_d)[GROUPS * b + 2 * (m % 2) + g, :, :,
                                                      512 * half:512 * half + 512]
                        sp.dma_start(dst.rearrange("a r t -> r a t"),
                                     parts[x_n % 4][g * GW:(g + 1) * GW]).then_inc(part_out[x_n % 4], 16)
                for k in range(4 * n, 4 * n + 4):
                    sp.wait_ge(job_dve, 6 * n + 4 + (k - 4 * n) // 2 + 1)
                    dst = v_d[GROUPS * b:GROUPS * (b + 1), :, k % TB, :].rearrange("g s f -> s g f")
                    sp.dma_start(dst, vt[:, k % 2].rearrange("p g h o d -> p g (h o d)")).then_inc(vt_out[k % 2], 16)
            for r in range(4):
                sp.wait_ge(part_out[r], 16 * 8)
            for r in range(2):
                sp.wait_ge(vt_out[r], 16 * 8)

            def load(s):
                at = s.n % BG
                for k, (pq, pk) in enumerate(zip(PIECES_Q, PIECES_K)):
                    rows = slice(k * HD, (k + 1) * HD)
                    sp.dma_start(qst[rows, s.u, :], q_d[at, pq].rearrange("(d h) t -> d (h t)", h=HG)).then_inc(stack_in[s.u], 16)
                    sp.dma_start(kst[rows, s.u, :], k_d[at, pk].rearrange("(d h) t -> d (h t)", h=HG)).then_inc(stack_in[s.u], 16)
                sp.dma_start(vst[:, s.u].rearrange("p j h d -> p (j h d)"),
                             v_d[at].rearrange("s j f -> s (j f)")).then_inc(stack_in[s.u], 16)

            def max_to_stack(s):
                sp.wait_ge(max_rows, s.n + 1)
                for a in range(3):
                    sp.dma_start(qst[KS + a:KS + a + 1, s.u, :].rearrange("p (r t) -> p r t", t=P),
                                 mrow[32 * a:32 * a + 32, :]).then_inc(max_in[s.u], 16)

            def context_out(s):
                sp.wait_ge(ctx_ready, 2 * s.n + 2)
                sp.dma_start(c_d[s.n % BG], cn[:].rearrange("p j d h -> p (j d h)")).then_inc(scratch[s.u], 16)

            def step(s, has_ctx, has_next, has_load):
                if has_load:
                    if has_ctx:
                        sp.wait_ge(prob_used, NQ * s.n)
                        sp.wait_ge(scratch[s.u], WBASE + 16 * CWRITES * (s.q - 1))
                    load(s.add(2))
                if has_ctx:
                    c = s.add(-1)
                    sp.wait_ge(scratch[c.u], WBASE + 16 * CWRITES * c.q)
                    context_out(c)
                    at = c.n % BG
                    sp.wait_ge(q_rows, 2 * c.n + 1)
                    for a in range(2):
                        sp.dma_start(q_d[at, a], qT1[a * GW:(a + 1) * GW, :]).then_inc(scratch[c.u], 16)
                    sp.wait_ge(q_rows, 2 * c.n + 2)
                    sp.dma_start(q_d[at, 2], qT2[:, :]).then_inc(scratch[c.u], 16)
                if has_next:
                    max_to_stack(s.add(1))

            for u in range(3):
                sp.sem_inc(scratch[u], WBASE)
            load(Step(0, 0))
            load(Step(0, 1))
            max_to_stack(Step(0, 0))
            over_steps(sp, step)

            last = Step(0, STEPS - 1)
            context_out(last)
            sp.wait_ge(scratch[0], WBASE + 16 * CWRITES * 8)
            sp.wait_ge(scratch[1], WBASE + 16 * CWRITES * 8)
            sp.wait_ge(scratch[2], WBASE + 16 * CWRITES * 7 + 16)
            sp.wait_ge(prob_used, NQ * STEPS)
            for at in range(BG):
                b, g = at // GROUPS, at % GROUPS
                sp.dma_start(cx[:, TB * b:TB * (b + 1), GW * g:GW * (g + 1)],
                             c_d[at].rearrange("p (j c) -> p j c", j=TB)).then_inc(ctx_in, 16)
            for k in range(NT):
                sp.wait_ge(fin_ready, k + 1)
                sp.dma_start(out.rearrange("b (j p) d -> p (b j) d", p=P)[:, k, :],
                             res[:, k % 4, :]).then_inc(stored[k % 4], 16)
            for r in range(4):
                sp.wait_ge(stored[r], 16 * NT // 4)

        @block.gpsimd
        def _(pool):
            count = [0]

            def link(ins, more=None):
                count[0] += 1
                ins.then_inc(pchain, 1)
                pool.wait_ge(pchain, count[0])

            link(pool.memset(identf[:], 0.0))
            pool.affine_select(out=identf[:], in_=identf[:], compare_op=ALU.not_equal, fill=1.0,
                               base=0, pattern=[[-1, P]], channel_multiplier=1).then_inc(consts, 1)
            pool.wait_ge(consts, 1)
            pool.tensor_copy(identb[:], identf[:]).then_inc(consts, 1)
            link(pool.memset(mask_l[:], 0.0))
            pool.affine_select(out=mask_l[:], in_=mask_l[:], compare_op=ALU.not_equal, fill=125.0,
                               base=0, pattern=[[-1, P]], channel_multiplier=1).then_inc(consts, 1)
            link(pool.memset(mask_r[:], 0.0))
            pool.affine_select(out=mask_r[:], in_=mask_r[:], compare_op=ALU.is_ge, fill=NEG / 125.0,
                               base=0, pattern=[[-1, P]], channel_multiplier=1).then_inc(consts, 1)
            pool.memset(vt[:], 1.0).then_inc(consts, 1)
            pool.wait_ge(idx_ready, 1)
            for k in range(NT):
                pool.indirect_dma_start(
                    out=h[:, k, :], out_offset=None, in_=tok_w,
                    in_offset=bass.IndirectOffsetOnAxis(ap=idx[:, k:k + 1], axis=0)).then_inc(gathered[k // 4], 16)

            def load_w(e, r):
                pool.dma_start(w1b[:, r], w1[e].rearrange("(k p) n -> p k n", p=P)).then_inc(w_loaded[r], 16)
                pool.dma_start(w2b[:, r], w2[e].rearrange("(k p) n -> p k n", p=P)).then_inc(w_loaded[r], 16)

            load_w(0, 0)
            load_w(1, 1)
            pool.wait_ge(consts, 5)
            for u in range(2):
                pool.memset(kst[KS:KM, u, :], 1.0).then_inc(ones_set, 1)
                pool.wait_ge(ones_set, u + 1)
            for r in range(4):
                pool.wait_ge(part_out[r], 16 * 8)
            pool.memset(kst[KS:KM, 2, :], 1.0).then_inc(ones_set, 1)
            pool.wait_ge(ones_set, 3)
            with pool.Fori(1, NEXP // 2) as i:
                for r in range(2):
                    pool.wait_ge(w_mul, 2 * i + r - 1)
                    load_w(2 * i + r, r)

            def step(s, has_ctx, has_next, has_load):
                for qd, (T, j, w, off, diag) in enumerate(QUADS):
                    if diag:
                        chunks, pitch = head_chunks(w)
                        for ci, heads in enumerate(chunks):
                            wait_alone(pool, exp_done, NC * s.n + CHUNKS_TO[qd] + ci + 1, pool_tally)
                            v = prob[:, qd % 3, 1024 * ci:1024 * ci + pitch * len(heads)]
                            v = v.rearrange("p (h c) -> p h c", c=pitch)[:, :, 0:P]
                            pool.affine_select(out=v, in_=v, compare_op=ALU.is_ge, fill=0.0, base=0,
                                               pattern=[[0, len(heads)], [1, P]],
                                               channel_multiplier=-1).then_inc(mask_done, 1)
                    if qd == SPLIT_QUAD and has_ctx:
                        c = s.add(-1)
                        cv = cn[:].rearrange("p j d h -> p j (d h)")
                        wait_alone(pool, ctx_ready, 2 * c.n + 2, pool_tally)
                        pool.tensor_copy(qn[:, :, 0, :], cv).then_inc(split_chain, 1)
                        wait_alone(pool, split_chain, 4 * c.n + 1, pool_tally)
                        pool.tensor_tensor(crest[:], cv, qn[:, :, 0, :], ALU.subtract).then_inc(split_chain, 1)
                        wait_alone(pool, split_chain, 4 * c.n + 2, pool_tally)
                        pool.tensor_copy(qn[:, :, 1, :], crest[:]).then_inc(split_chain, 1)
                        wait_alone(pool, split_chain, 4 * c.n + 3, pool_tally)
                        pool.tensor_tensor(qn[:, :, 2, :], crest[:], qn[:, :, 1, :], ALU.subtract).then_inc(split_chain, 1)

            over_steps(pool, step)

        @block.scalar
        def _(act):
            def make_mid(x_n):
                act.wait_ge(x_rest, x_n + 1)
                act.copy(parts[x_n % 4][:, 1, :], rs[:, x_n % 3, :]).then_inc(x_mid, 1)

            x_n = 0
            for k, (kind, a, c) in enumerate(jobs):
                if kind == "turn" and a % 2 == 0:
                    act.wait_ge(var_ready, a // 2 + 1)
                    act.activation(std[:, 2 * a:2 * a + 4], var[:, 2 * a:2 * a + 4],
                                   ACT.Sqrt).then_inc(std_ready, 1)
                if not by_dve[k]:
                    act.wait_ge(job_done, k + 1)
                    bank = ps[:, k % RING, :]
                    if kind == "wqkv":
                        w = 512 if c == 0 else 256
                        act.copy(wT[:, a, 512 * c:512 * c + w], bank[:, 0:w]).then_inc(job_act, 1)
                    elif kind == "wo":
                        act.copy(woT[:].rearrange("p k n -> p (k n)"), bank).then_inc(job_act, 1)
                    else:
                        act.copy(xT[:, :, 256 * a:256 * a + 256],
                                 bank.rearrange("p (k n) -> p k n", k=2)).then_inc(job_act, 1)
                if kind == "qk":
                    act.wait_ge(job_dve, sum(by_dve[:k + 1]))
                    if x_n >= 4:
                        act.wait_ge(part_out[x_n % 4], 32 * (x_n // 4))
                    act.copy(parts[x_n % 4][:, 0, :], xs[:, x_n % 3, :]).then_inc(x_hi, 1)
                    if a >= 1:
                        make_mid(x_n - 1)
                    x_n += 1
                if kind == "v" and a % 2 == 0:
                    make_mid(x_n - 1)

            def w_copies(e):
                act.wait_ge(w_turned, e + 1)
                for k in range(2):
                    act.copy(w1T[:, 4 * k:4 * k + 2, :].rearrange("p a n -> p (a n)"),
                             ps[:, 2 * k, :]).then_inc(w_evac_act, 1)

            with act.Fori(0, NEXP) as e:
                w_copies(e)

            def copy_context(s, T):
                act.wait_ge(prob_used, NQ * s.n + (4 if T == 0 else NQ))
                act.copy(cT[:, T, :], ps[:, PV_BANK, :]).then_inc(pv_copied, 1)

            def copy_max(s):
                act.wait_ge(max_turned, s.n + 1)
                if not (isinstance(s.n, int) and s.n == 0):
                    p = s.add(-1)
                    act.wait_ge(max_in[p.u], 48 * (p.q + 1))
                act.copy(mrow[0:96, :], misc_bf[0:96, 0:P]).then_inc(max_rows, 1)

            def step(s, has_ctx, has_next, has_load):
                for qd, (T, j, w, off, diag) in enumerate(QUADS):
                    chunks, pitch = head_chunks(w)
                    if not (isinstance(s.n, int) and NQ * s.n + qd < 3):
                        act.wait_ge(prob_used, NQ * s.n + qd - 2)
                    for ci, heads in enumerate(chunks):
                        ch = CHUNKS_TO[qd] + ci
                        act.wait_ge(st_ready, NC * s.n + ch + 1)
                        n = len(heads)
                        src = ps[:, ST_BANK + 2 * (ch % 2):ST_BANK + 2 * (ch % 2) + 2, :].rearrange("p a c -> p (a c)")
                        src = src[:, 0:n * pitch].rearrange("p (h c) -> p h c", c=pitch)[:, :, 0:w]
                        dst = prob[:, qd % 3, 1024 * ci:1024 * ci + n * pitch]
                        dst = dst.rearrange("p (h c) -> p h c", c=pitch)[:, :, 0:w]
                        act.activation(dst, src, ACT.Exp).then_inc(exp_done, 1)
                    if qd == EVAC1_QUAD and has_ctx:
                        copy_context(s.add(-1), 1)
                    if qd == EVAC0_QUAD:
                        copy_context(s, 0)
                    if qd in QT_QUAD and has_ctx:
                        half = QT_QUAD.index(qd)
                        act.wait_ge(q_turned, 2 * s.n - 1 + half)
                        if half == 0:
                            act.copy(qT1[:], misc_bf).then_inc(q_rows, 1)
                        else:
                            act.copy(qT2[:], misc_bf[0:GW, :]).then_inc(q_rows, 1)
                    if qd == MAX_QUAD and has_next:
                        copy_max(s.add(1))

            copy_max(Step(0, 0))
            over_steps(act, step)
            copy_context(Step(0, STEPS - 1), 1)

            for k in range(8):
                act.wait_ge(e_job, k + 1)
                act.copy(xT[:, :, 256 * k:256 * k + 256],
                         ps[:, k % 2, :].rearrange("p (k n) -> p k n", k=2)).then_inc(e_act, 1)
            for n in range(4):
                act.wait_ge(e_var, n + 1)
                act.activation(std[:, 4 * n:4 * n + 4], var[:, 4 * n:4 * n + 4], ACT.Sqrt).then_inc(e_std, 1)
                for k in (8 + 2 * n, 9 + 2 * n):
                    act.wait_ge(e_job, k + 1)
                    act.copy(xT[:, :, 256 * (k - 8):256 * (k - 8) + 256],
                             ps[:, k % 2, :].rearrange("p (k n) -> p k n", k=2)).then_inc(e_act, 1)

        @block.vector
        def _(dve):
            count = [0]

            def link(ins):
                count[0] += 1
                ins.then_inc(dchain, 1)
                dve.wait_ge(dchain, count[0])

            def norm_stats(n, ready):
                for k in range(4 * n, 4 * n + 4):
                    last = dve.bn_stats(stats[:, k, :], h[:, k, :])
                link(last)
                for k in range(4 * n, 4 * n + 4):
                    last = dve.bn_aggr(mv[:, k, :], stats[:, k, :])
                link(last)
                dve.tensor_scalar_add(var[:, 4 * n:4 * n + 4], mv[:, 4 * n:4 * n + 4, 1], EPS).then_inc(ready, 1)

            def normalise(n, root, dst):
                dve.wait_ge(root, n + 1)
                link(dve.reciprocal(rstd[:, 4 * n:4 * n + 4], std[:, 4 * n:4 * n + 4]))
                for k in range(4 * n, 4 * n + 4):
                    last = dve.tensor_scalar(dst[:, k % dst.shape[1], :], h[:, k, :], mv[:, k, 0:1], rstd[:, k:k + 1],
                                             ALU.subtract, ALU.mult)
                return last

            dve.wait_ge(in_x, 32)
            dve.tensor_copy(idx_f[:], idx_row[:]).then_inc(rows_ready, 1)
            dve.tensor_copy(bias_p[:].rearrange("m (g d h) -> m g d h", d=HD, h=HG),
                            bias_row[:].rearrange("m (g h d) -> m g d h", h=HG, d=HD)).then_inc(rows_ready, 1)
            dve.wait_ge(rows_turned, 1)
            dve.tensor_copy(idx[:], misc[:, 0:NT]).then_inc(idx_ready, 1)
            link(dve.tensor_copy(bias_qk[:], misc[:, NT:NT + 4]))
            link(dve.memset(w12[:], 0.0))
            link(dve.memset(mx[:], ROW_LOW))
            dve.wait_ge(in_w, 16 * 10)
            for o in range(2):
                last = dve.tensor_copy(owp[:, o, :].rearrange("p (g d h) -> p g d h", d=HD, h=HG),
                                       own[:, o, :].rearrange("p (g h d) -> p g d h", d=HD, h=HG))
            last.then_inc(owp_ready, 1)
            dve.wait_ge(in_b, 16 * 2)

            def make_rest(x_n):
                dve.wait_ge(x_hi, x_n + 1)
                dve.tensor_tensor(rs[:, x_n % 3, :], xs[:, x_n % 3, :], parts[x_n % 4][:, 0, :],
                                  ALU.subtract).then_inc(x_rest, 1)

            def make_low(x_n):
                dve.wait_ge(x_mid, x_n + 1)
                dve.tensor_tensor(parts[x_n % 4][:, 2, :], rs[:, x_n % 3, :], parts[x_n % 4][:, 1, :],
                                  ALU.subtract).then_inc(x_lo, 1)

            x_n = 0
            for k, (kind, a, c) in enumerate(jobs):
                if kind == "turn" and a % 2 == 0:
                    n = a // 2
                    dve.wait_ge(gathered[n], 64)
                    norm_stats(n, var_ready)
                    if n >= 1:
                        dve.wait_ge(job_done, jobs.index(("turn", 2 * n - 1, 0)) + 1)
                    normalise(n, std_ready, hn).then_inc(hn_ready, 1)
                if kind == "qk":
                    dve.wait_ge(job_done, k + 1)
                    scale = 1.0 if a < 2 else KEY_SCALE
                    dve.tensor_scalar(xs[:, x_n % 3, :], ps[:, k % RING, :], bias_qk[:, a:a + 1], scale,
                                      ALU.add, ALU.mult).then_inc(job_dve, 1)
                    if a >= 1:
                        make_rest(x_n - 1)
                    if a >= 2:
                        make_low(x_n - 2)
                    x_n += 1
                if kind == "v":
                    if a % 2 == 0:
                        make_rest(x_n - 1)
                        make_low(x_n - 2)
                    else:
                        make_low(x_n - 1)
                    dve.wait_ge(job_done, k + 1)
                    for r in range(2):
                        blk = 2 * a + r
                        if a == 0:
                            dve.wait_ge(consts, 5)
                        else:
                            dve.wait_ge(vt_out[r], 16 * a)
                        last = dve.tensor_tensor(
                            vt[:, r, :, :, 0, :],
                            ps[:, k % RING, 256 * r:256 * r + 256].rearrange("p (g h d) -> p g h d", g=GROUPS, h=HG),
                            bias_v[:].rearrange("p (g h d) -> p g h d", g=GROUPS, h=HG), ALU.add)
                    last.then_inc(job_dve, 1)
            for k in range(NT):
                last = dve.tensor_tensor(h[:, k, :], h[:, k, :], bias_o[:], ALU.add)
            link(last)

            with dve.Fori(0, NEXP) as e:
                dve.wait_ge(w_turned, e + 1)
                for k in range(2):
                    dve.tensor_copy(w1T[:, 4 * k + 2:4 * k + 4, :].rearrange("p a n -> p (a n)"),
                                    ps[:, 2 * k + 1, :]).then_inc(w_evac_dve, 1)
                dve.wait_ge(w_mul, e + 1)
                dve.tensor_tensor(w12[:], w12[:], ps[:, 4:6, 0:D], ALU.add).then_inc(w_acc, 1)

            def row_max(s, c):
                i, half, heads, k0, w, diag = NAT[c]
                dve.wait_ge(nat_ready, NN * s.n + c + 1)
                if c == 0 and not (isinstance(s.n, int) and s.n == 0):
                    dve.wait_ge(max_chain, 5 * s.n)
                src = ps[:, NAT_BANK + c % 2, 0:w * len(heads)].rearrange("p (h c) -> p h c", c=w)
                dve.tensor_reduce(mx[:, heads[0]:heads[-1] + 1, i, half], src, AX.X, ALU.max).then_inc(nat_used, 1)

            def finish_max(s):
                n5 = 5 * s.n
                dve.wait_ge(nat_used, NN * (s.n + 1))
                dve.tensor_reduce(negm[:], mx[:].rearrange("p h i c -> p (h i) c"), AX.X, ALU.max,
                                  negate=True).then_inc(max_chain, 1)
                dve.wait_ge(max_chain, n5 + 1)
                if not (isinstance(s.n, int) and s.n == 0):
                    dve.wait_ge(max_turned, s.n)
                dve.tensor_copy(msp[:, 0, :], negm[:]).then_inc(max_chain, 1)
                dve.wait_ge(max_chain, n5 + 2)
                dve.tensor_tensor(mrest[:], negm[:], msp[:, 0, :], ALU.subtract).then_inc(max_chain, 1)
                dve.wait_ge(max_chain, n5 + 3)
                dve.tensor_copy(msp[:, 1, :], mrest[:]).then_inc(max_chain, 1)
                dve.wait_ge(max_chain, n5 + 4)
                dve.tensor_tensor(msp[:, 2, :], mrest[:], msp[:, 1, :], ALU.subtract).then_inc(max_chain, 1)

            def divide(s, T):
                dve.wait_ge(ctx_turned, 2 * s.n + T + 1)
                tile = misc.rearrange("p (j h c) -> p j h c", j=4, h=HG)
                dve.reciprocal(rden[:].rearrange("p (j h) -> p j h", j=4), tile[:, :, :, HD]).then_inc(den_ready, 1)
                dve.wait_ge(den_ready, 2 * s.n + T + 1)
                if T == 0 and not (isinstance(s.n, int) and s.n == 0):
                    p = s.add(-1)
                    dve.wait_ge(scratch[p.u], WBASE + 16 * CWRITES * (p.q + 1))
                dve.tensor_tensor(
                    cn[:, 4 * T:4 * T + 4].rearrange("p j d h -> p j h d"), tile[:, :, :, 0:HD],
                    rden[:].rearrange("p (j h) -> p j h", j=4).unsqueeze(3).broadcast_to([P, 4, HG, HD]),
                    ALU.mult).then_inc(ctx_ready, 1)

            def step(s, has_ctx, has_next, has_load):
                for qd in range(NQ):
                    if has_next:
                        for c in NAT_AT[qd]:
                            row_max(s.add(1), c)
                    if qd in CTX_QUAD and has_ctx:
                        divide(s.add(-1), CTX_QUAD.index(qd))
                    if qd == NAT_QUADS - 1 and has_next:
                        finish_max(s.add(1))

            for c in range(NN):
                row_max(Step(0, 0), c)
            finish_max(Step(0, 0))
            over_steps(dve, step)
            for T in range(2):
                divide(Step(0, STEPS - 1), T)

            for n in range(4):
                for k in range(4 * n, 4 * n + 4):
                    dve.wait_ge(h1_ready, k + 1)
                    last = dve.tensor_tensor(h[:, k, :], h[:, k, :], ps[:, 2 + k % 2, 0:D], ALU.add)
                    last.then_inc(e_dve, 1)
                dve.wait_ge(e_dve, 4 * n + 4)
                norm_stats(n, e_var)
                normalise(n, e_std, hn2).then_inc(e_hn, 1)
            for k in range(NT):
                dve.wait_ge(h1_ready, NT + k + 1)
                if k >= 4:
                    dve.wait_ge(stored[k % 4], 16 * (k // 4))
                dve.tensor_tensor(res[:, k % 4, :], h[:, k, :], ps[:, 2 + k % 2, 0:D], ALU.add).then_inc(fin_ready, 1)

        @block.tensor
        def _(pe):
            pe.wait_ge(consts, 1)
            pe.wait_ge(rows_ready, 2)
            pe.transpose(misc[:, 0:NT], idx_f[:], identf[0:NT, 0:NT])
            pe.transpose(misc[:, NT:NT + 4], bias_p[:], identf[0:4, 0:4]).then_inc(rows_turned, 1)
            for k, (kind, a, c) in enumerate(jobs):
                if k >= RING:
                    copied(pe, k - RING)
                bank = ps[:, k % RING, :]
                if kind == "wqkv":
                    pe.wait_ge(in_w, 16 * 10)
                    for x_m, m in enumerate(range(4 * c, 4 * c + (4 if c == 0 else 2))):
                        last = pe.transpose(bank[:, x_m * P:(x_m + 1) * P], wn[:, m, a * P:(a + 1) * P], identf[:])
                elif kind == "wo":
                    pe.wait_ge(owp_ready, 1)
                    for kc in range(2):
                        for o in range(2):
                            last = pe.transpose(bank[:, (2 * kc + o) * P:(2 * kc + o + 1) * P],
                                                owp[:, o, kc * P:(kc + 1) * P], identf[:])
                elif kind == "turn":
                    pe.wait_ge(hn_ready, a // 2 + 1)
                    for kc in range(2):
                        for r in range(2):
                            last = pe.transpose(bank[:, 256 * kc + P * r:256 * kc + P * (r + 1)],
                                                hn[:, (2 * a + r) % 4, kc * P:(kc + 1) * P], identf[:])
                elif kind == "qk":
                    copied(pe, max(j for j in range(k) if jobs[j][0] == "turn" and jobs[j][1] <= 2 * c + 1))
                    for kc in range(2):
                        last = pe.matmul(bank, wT[:, kc, a * P:(a + 1) * P], xT[:, kc, 512 * c:512 * c + 512],
                                         start=(kc == 0), stop=(kc == 1))
                else:
                    for r in range(2):
                        blk = 2 * a + r
                        for kc in range(2):
                            last = pe.matmul(bank[:, 256 * r:256 * r + 256], xT[:, kc, blk * P:(blk + 1) * P],
                                             wT[:, kc, 2 * D:3 * D], start=(kc == 0), stop=(kc == 1))
                last.then_inc(job_done, 1)

            for k in range(len(jobs) - RING, len(jobs)):
                copied(pe, k)

            def turn_w(e, r, uses):
                pe.wait_ge(w_loaded[r], 32 * uses)
                for k in range(8):
                    for kc in range(2):
                        last = pe.transpose(ps[:, k // 2, 256 * (k % 2) + P * kc:256 * (k % 2) + P * (kc + 1)],
                                            w1b[:, r, kc, P * k:P * (k + 1)], identf[:])
                last.then_inc(w_turned, 1)

            def mul_w(e, r):
                pe.wait_ge(w_evac_act, 2 * e + 2)
                pe.wait_ge(w_evac_dve, 2 * e + 2)
                for m in range(2):
                    for k in range(8):
                        last = pe.matmul(ps[:, 4 + m, 0:D], w1T[:, k, m * P:(m + 1) * P], w2b[:, r, k, :],
                                         start=(k == 0), stop=(k == 7))
                last.then_inc(w_mul, 1)

            with pe.Fori(0, NEXP // 2) as i:
                for r in range(2):
                    turn_w(2 * i + r, r, i + 1)
                    mul_w(2 * i + r, r)
                    pe.wait_ge(w_acc, 2 * i + r + 1)

            def row_scores(s, c):
                i, half, heads, k0, w, diag = NAT[c]
                if not (isinstance(s.n, int) and NN * s.n + c < 2):
                    pe.wait_ge(nat_used, NN * s.n + c - 1)
                for x_h, a in enumerate(heads):
                    o = ps[:, NAT_BANK + c % 2, x_h * w:(x_h + 1) * w]
                    last = pe.matmul(o, qst[0:KS, s.u, S * a + P * i:S * a + P * (i + 1)],
                                     kst[0:KS, s.u, S * a + k0:S * a + k0 + w], start=True, stop=not diag)
                    if diag:
                        last = pe.matmul(o[:, w - P:w], mask_l[:], mask_r[:], start=False, stop=True)
                last.then_inc(nat_ready, 1)

            def key_scores(s, qd):
                T, j, w, off, diag = QUADS[qd]
                chunks, pitch = head_chunks(w)
                for ci, heads in enumerate(chunks):
                    ch = CHUNKS_TO[qd] + ci
                    if not (isinstance(s.n, int) and NC * s.n + ch < 2):
                        pe.wait_ge(exp_done, NC * s.n + ch - 1)
                    slot = ps[:, ST_BANK + 2 * (ch % 2):ST_BANK + 2 * (ch % 2) + 2, :].rearrange("p a c -> p (a c)")
                    for x_h, a in enumerate(heads):
                        t0 = S * a + 512 * T + off
                        last = pe.matmul(slot[:, x_h * pitch:x_h * pitch + w],
                                         kst[0:KM, s.u, S * a + P * j:S * a + P * (j + 1)],
                                         qst[0:KM, s.u, t0:t0 + w], start=True, stop=True)
                    last.then_inc(st_ready, 1)

            def values(s, qd):
                T, j, w, off, diag = QUADS[qd]
                chunks, pitch = head_chunks(w)
                pe.wait_ge(exp_done, NC * s.n + CHUNKS_TO[qd + 1])
                if diag:
                    pe.wait_ge(mask_done, NM * s.n + MASKS_TO[qd + 1])
                if j == 0 and not (isinstance(s.n, int) and 2 * s.n + T == 0):
                    pe.wait_ge(pv_copied, 2 * s.n + T)
                for ci, heads in enumerate(chunks):
                    for x_h, a in enumerate(heads):
                        c0 = 1024 * ci + x_h * pitch
                        last = pe.matmul(ps[32 * a:32 * a + 32, PV_BANK, off:off + w], vst[:, s.u, j, a, :],
                                         prob[:, qd % 3, c0:c0 + w], start=(j == 0), stop=(j == 4 * T + 3))
                last.then_inc(prob_used, 1)

            def turn_max(s):
                pe.wait_ge(max_chain, 5 * s.n + 5)
                pe.transpose(misc_bf[0:96, 0:P], msp[:].rearrange("p a r -> p (a r)"), identb[:]).then_inc(max_turned, 1)

            def turn_context(s, T):
                pe.wait_ge(pv_copied, 2 * s.n + T + 1)
                if T == 0 and isinstance(s.n, int) and s.n == STEPS - 1:
                    pe.wait_ge(q_rows, 2 * s.n)
                elif T == 0:
                    pe.wait_ge(max_rows, s.n + 2)
                else:
                    pe.wait_ge(ctx_ready, 2 * s.n + 1)
                for j in range(4):
                    last = pe.transpose(misc[:, P * j:P * (j + 1)], cT[:, T, P * j:P * (j + 1)], identf[:])
                last.then_inc(ctx_turned, 1)

            def turn_queries(s, half):
                if half == 0:
                    pe.wait_ge(split_chain, 4 * s.n + 4)
                else:
                    wait_alone(pe, q_rows, 2 * s.n + 1, pe_tally)
                cols = slice(0, P) if half == 0 else slice(P, P + GW)
                rows = P if half == 0 else GW
                for j in range(TB):
                    last = pe.transpose(misc_bf[0:rows, P * j:P * (j + 1)],
                                        qn[:, j].rearrange("p a r -> p (a r)")[:, cols], identb[:])
                last.then_inc(q_turned, 1)

            def step(s, has_ctx, has_next, has_load):
                nxt = s.add(1)
                for qd in range(NQ):
                    if qd == 0:
                        if has_ctx:
                            values(s.add(-1), NQ - 1)
                        if has_next:
                            pe.wait_ge(stack_in[nxt.u], 16 * LOADS * (nxt.q + 1))
                            for c in NAT_AT[0]:
                                row_scores(nxt, c)
                        pe.wait_ge(max_in[s.u], 48 * (s.q + 1))
                    key_scores(s, qd)
                    if qd > 0:
                        if has_next:
                            for c in NAT_AT[qd]:
                                row_scores(nxt, c)
                        values(s, qd - 1)
                    if has_ctx and qd in CTX_QUAD:
                        turn_context(s.add(-1), CTX_QUAD.index(qd))
                    if has_ctx and qd in QT_QUAD:
                        turn_queries(s.add(-1), QT_QUAD.index(qd))
                    if qd == MAX_QUAD and has_next:
                        if has_ctx:
                            pe.wait_ge(q_rows, 2 * s.n)
                        else:
                            pe.wait_ge(max_rows, 1)
                        turn_max(nxt)

            pe.wait_ge(consts, 5)
            pe.wait_ge(stack_in[0], 16 * LOADS)
            for c in range(NN):
                row_scores(Step(0, 0), c)
            turn_max(Step(0, 0))
            pe.wait_ge(ones_set, 3)
            over_steps(pe, step)
            last_step = Step(0, STEPS - 1)
            values(last_step, NQ - 1)
            for T in range(2):
                turn_context(last_step, T)

            pe.wait_ge(ctx_in, 16 * BG)
            for k in range(8):
                if k >= 2:
                    pe.wait_ge(e_act, k - 1)
                for kc in range(2):
                    for r in range(2):
                        blk = 2 * k + r
                        last = pe.transpose(ps[:, k % 2, 256 * kc + P * r:256 * kc + P * (r + 1)],
                                            cx[:, blk, kc * P:(kc + 1) * P], identf[:])
                last.then_inc(e_job, 1)

            def product(k, w, turned):
                pe.wait_ge(e_act, turned)
                for kc in range(2):
                    last = pe.matmul(ps[:, 2 + k % 2, 0:D], xT[:, kc, k * P:(k + 1) * P], w[:, kc, :],
                                     start=(kc == 0), stop=(kc == 1))
                last.then_inc(h1_ready, 1)

            def turn_norm(n):
                pe.wait_ge(e_hn, n + 1)
                for k in (2 * n, 2 * n + 1):
                    pe.wait_ge(e_act, 8 + k - 1)
                    for kc in range(2):
                        for r in range(2):
                            last = pe.transpose(ps[:, k % 2, 256 * kc + P * r:256 * kc + P * (r + 1)],
                                                hn2[:, 2 * k + r, kc * P:(kc + 1) * P], identf[:])
                    last.then_inc(e_job, 1)

            for n in range(4):
                for k in range(4 * n, 4 * n + 4):
                    if k >= 2:
                        pe.wait_ge(e_dve, k - 1)
                    product(k, woT, k // 2 + 1)
                if n >= 1:
                    turn_norm(n - 1)
            turn_norm(3)
            for k in range(NT):
                if k >= 2:
                    pe.wait_ge(fin_ready, k - 1)
                else:
                    pe.wait_ge(e_dve, NT)
                product(k, w12, 8 + k // 2 + 1)


def kernel(**inputs):
    import numpy as np
    import concourse.bacc as bacc
    from concourse.bass_utils import run_bass_kernel_spmd

    nc = bacc.Bacc("TRN2", target_bir_lowering=False, num_devices=1)
    names = ["x", "L0_tok_W", "L0_attn_Wqkv_w", "L0_attn_Wqkv_b", "L0_attn_out_w", "L0_attn_out_b",
             "L0_ffn_w1", "L0_ffn_w2"]
    arrays, args = {}, []
    for name in names:
        a = np.ascontiguousarray(inputs[name])
        arrays[f"in_{name}"] = a
        args.append(nc.dram_tensor(f"in_{name}", a.shape, mybir.dt.from_np(a.dtype), kind="ExternalInput").ap())
    args.append(nc.dram_tensor("out", (B, S, D), F32, kind="ExternalOutput").ap())
    layer(nc, *args)
    return run_bass_kernel_spmd(nc, [arrays], core_ids=[0]).results[0]["out"]
```

```python
from contextlib import ExitStack

import concourse.bass as bass
from concourse import mybir

ACT = mybir.ActivationFunctionType
ALU = mybir.AluOpType
AX = mybir.AxisListType
F32 = mybir.dt.float32
BF16 = mybir.dt.bfloat16
I32 = mybir.dt.int32

P = 128
B = 2
S = 1024
D = 256
HD = 16
NEXP, N_FF = 8, 1024
ROUNDS = 3
HG = 4
GROUPS = D // (HD * HG)
GW = HD * HG
BG = B * GROUPS
STEPS = ROUNDS * BG
TB = S // P
NT = B * TB
KS = 96
KM = 99
EPS = 1e-5
KEY_SCALE = HD ** -0.5
NEG = -10000.0
ROW_LOW = -3.0e38

NAT = []
for _i in range(TB):
    for _c in range(1 if _i < 4 else 2):
        _w = P * (_i + 1) if _i < 4 else (512 if _c == 0 else P * (_i - 3))
        _nh = 4 if _w == 128 else 2 if _w == 256 else 1
        for _h in range(0, HG, _nh):
            NAT.append((_i, _c, list(range(_h, _h + _nh)), 512 * _c, _w, _i < 4 or _c == 1))
NN = len(NAT)

QUADS = []
for _t in range(2):
    for _j in range(4 * (_t + 1)):
        _k = max(0, _j - 4 * _t)
        QUADS.append((_t, _j, 512 - P * _k, P * _k, _j >= 4 * _t))
NQ = len(QUADS)


def head_chunks(w):
    return ([[0, 1], [2, 3]], 512) if w > 256 else ([[0, 1, 2, 3]], w)


CHUNKS_TO = [0]
MASKS_TO = [0]
for _q in QUADS:
    CHUNKS_TO.append(CHUNKS_TO[-1] + len(head_chunks(_q[2])[0]))
    MASKS_TO.append(MASKS_TO[-1] + len(head_chunks(_q[2])[0]) * _q[4])
NC, NM = CHUNKS_TO[-1], MASKS_TO[-1]



SLACK = 0


def plan_step():
    frame = [("pv", -2), ("st", 0, 0), ("pv", -1), ("st", 0, 1), ("copy", 1), ("st", 1, 0), ("st", 1, 1), ("pv", 0), ("ctx", 0),
             ("st", 2, 0), ("pv", 1), ("ctx", 1), ("st", 3, 0), ("pv", 2), ("hi",),
             ("st", 4, 0), ("st", 4, 1), ("pv", 3), ("rest",), ("copy", 0), ("mid",),
             ("st", 5, 0), ("st", 5, 1), ("pv", 4), ("low",), ("st", 6, 0), ("st", 6, 1), ("pv", 5), ("qt", 0),
             ("st", 7, 0), ("st", 7, 1), ("pv", 6), ("qt", 1), ("st", 8, 0), ("st", 8, 1), ("pv", 7),
             ("st", 9, 0), ("st", 9, 1), ("pv", 8), ("st", 10, 0), ("pv", 9), ("st", 11, 0)]
    plan, pe, c = [], 0, 0
    read = [0, 0]
    for item in frame:
        while c < len(NAT) and pe + SLACK >= read[-2]:
            pe = max(pe, read[-2])
            cols = len(NAT[c][2]) * NAT[c][4]
            pe += 0.42 * cols + (55 if NAT[c][5] else 0) * len(NAT[c][2])
            read.append(max(read[-1], pe) + 65 + 1.04 * cols)
            plan.append(("nat", c))
            c += 1
        if item[0] == "st":
            pe += 0.42 * QUADS[item[1]][2] * len(head_chunks(QUADS[item[1]][2])[0][0])
        if item[0] == "pv":
            pe += 1.83 * QUADS[item[1]][2]
        if item[0] in ("ctx", "qt"):
            pe += 450
        if item[0] == "ctx":
            read[-1] += 500
        plan.append(item)
    plan += [("nat", k) for k in range(c, len(NAT))]
    plan.insert(plan.index(("st", 8, 1)) + 1, ("max", 0))
    plan.insert(plan.index(("st", 0, 1)) + 1, ("max", 1))
    plan.insert(plan.index(("low",)) + 1, ("parts", 0))
    plan.append(("parts", 1))
    return plan


PLAN = plan_step()
NAT_HALF = sum(c[0] < 4 for c in NAT)

PIECES_Q = (0, 1, 2, 0, 1, 0)
PIECES_K = (0, 0, 0, 1, 1, 2)
LOADS = len(PIECES_Q) + len(PIECES_K) + 1
CWRITES = 4
PROJ_WRITES = 48
WBASE = PROJ_WRITES // 3 * 16


def wait_alone(eng, sem, value, tally):
    eng.wait_ge(sem, value)
    eng.sem_inc(tally, 1)


class Step:

    def __init__(self, i, off):
        self.i, self.off = i, off
        self.n = 3 * i + off
        self.u = off % 3
        self.q = i + off // 3

    def add(self, d):
        return Step(self.i, self.off + d)


def over_steps(eng, step):
    step(Step(0, 0), has_ctx=False, has_next=True, has_load=True)
    turns = (STEPS - 3) // 3
    with eng.Fori(0, turns) as i:
        for k in range(3):
            step(Step(i, 1 + k), has_ctx=True, has_next=True, has_load=True)
    step(Step(turns, 1), has_ctx=True, has_next=True, has_load=False)
    step(Step(turns, 2), has_ctx=True, has_next=False, has_load=False)


def layer(nc, x, tok_w, wqkv, bqkv, out_w, out_b, w1, w2, out):
    with ExitStack() as ctx:
        def sb(name, shape, dt):
            return ctx.enter_context(nc.sbuf_tensor(name, shape, dt))

        def sem(name):
            return ctx.enter_context(nc.semaphore(name))

        q_d = nc.dram_tensor("q_parts", [BG, 3, 2, GW, 512], BF16, kind="Internal").ap()
        k_d = nc.dram_tensor("k_parts", [BG, 3, GW, S], BF16, kind="Internal").ap()
        v_d = nc.dram_tensor("v_ones", [BG, P, TB, 2 * GW], F32, kind="Internal").ap()
        c_d = nc.dram_tensor("context", [BG, P, TB * GW], F32, kind="Internal").ap()

        ps = ctx.enter_context(nc.psum_tensor("ps", [P, 8, 512], F32))
        ST_BANK, NAT_BANK, PV_BANK, MISC_BANK = 0, 4, 6, 7
        misc = ps[:, MISC_BANK, :]
        misc_bf = misc.bitcast(BF16)

        h = sb("h", [P, NT, D], F32)
        xT = sb("xT", [P, 2, B * S], F32)
        wn = sb("wn", [P, 6, D], F32)
        wT = sb("wT", [P, 2, 3 * D], F32)
        own = sb("own", [P, 2, D], F32)
        owp = sb("owp", [P, 2, D], F32)
        woT = sb("woT", [P, 2, D], F32)
        bias_qk = sb("bias_qk", [P, 4], F32)
        bias_v = sb("bias_v", [P, D], F32)
        bias_o = sb("bias_o", [P, D], F32)
        idx_row = sb("idx_row", [NT, P], I32)
        idx_f = sb("idx_f", [NT, P], F32)
        idx = sb("idx", [P, NT], I32)
        bias_row = sb("bias_row", [4, P], F32)
        bias_p = sb("bias_p", [4, P], F32)
        identf = sb("identf", [P, P], F32)
        identb = sb("identb", [P, P], BF16)
        mask_l = sb("mask_l", [P, P], BF16)
        mask_r = sb("mask_r", [P, P], BF16)
        stats = sb("stats", [P, NT, 6], F32)
        mv = sb("mv", [P, NT, 2], F32)
        var = sb("var", [P, NT], F32)
        std = sb("std", [P, NT], F32)
        rstd = sb("rstd", [P, NT], F32)
        hn = sb("hn", [P, 4, D], F32)
        vt = sb("vt", [P, 4, GROUPS, HG, 2, HD], F32)
        w12 = sb("w12", [P, 2, D], F32)
        work = sb("work", [P, 10240], F32)
        qst = sb("qst", [P, 3, HG * S], BF16)
        kst = sb("kst", [P, 3, HG * S], BF16)
        vst = sb("vst", [P, 3, TB, HG, 2 * HD], F32)
        mx = sb("mx", [P, HG, TB, 2], F32)
        negm = sb("negm", [P, 2, HG * 4], F32)
        mrest = sb("mrest", [P, 2, HG * 4], F32)
        msp = sb("msp", [P, 2, 3, HG * 4], BF16)
        mrow = sb("mrow", [48, 2, P], BF16)
        cT = sb("cT", [P, 2, 512], F32)
        rden = sb("rden", [P, 16], F32)
        cn = sb("cn", [P, TB, HD, HG], F32)
        crest = sb("crest", [P, TB, GW], F32)
        qn = sb("qn", [P, TB, 3, GW], BF16)
        qT1 = sb("qT1", [P, S], BF16)
        qT2 = sb("qT2", [GW, S], BF16)

        w1b = work[:, 0:4096].rearrange("p (u k n) -> p u k n", u=2, k=2)
        w2b = work[:, 4096:8192].rearrange("p (u k n) -> p u k n", u=2, k=8)
        w1T = work[:, 8192:10240].rearrange("p (k n) -> p k n", k=8)
        prob = work[:, 0:6144].rearrange("p (s c) -> p s c", s=3)
        cx = work[:, 6144:10240].rearrange("p (k c) -> p k c", k=NT)
        hn2 = cx
        res = work[:, 1024:2048].rearrange("p (k n) -> p k n", k=4)
        xs = qst[:, 0, 0:3072].bitcast(F32).rearrange("p (r n) -> p r n", r=3)
        rs = qst[:, 1, 0:3072].bitcast(F32).rearrange("p (r n) -> p r n", r=3)
        parts = [t[:, 2, 1536 * r:1536 * (r + 1)].rearrange("p (a n) -> p a n", a=3)
                 for t in (qst, kst) for r in range(2)]

        in_x, in_w, in_b = sem("in_x"), sem("in_w"), sem("in_b")
        consts, ones_set = sem("consts"), sem("ones_set")
        rows_ready, rows_turned, idx_ready = sem("rows_ready"), sem("rows_turned"), sem("idx_ready")
        gathered = [sem(f"gathered{n}") for n in range(4)]
        dchain = sem("dve_chain")
        pchain = sem("pool_chain")
        var_ready, std_ready = sem("var_ready"), sem("std_ready")
        hn_ready = sem("hn_ready")
        owp_ready = sem("owp_ready")
        job_done, job_act, job_dve = sem("job_done"), sem("job_act"), sem("job_dve")
        x_hi, x_rest, x_mid, x_lo = sem("x_hi"), sem("x_rest"), sem("x_mid"), sem("x_lo")
        part_out = [sem(f"part_out{r}") for r in range(4)]
        vt_out = [sem(f"vt_out{r}") for r in range(4)]
        w_loaded = [sem(f"w_loaded{r}") for r in range(2)]
        w_turned, w_evac_act, w_evac_dve = sem("w_turned"), sem("w_evac_act"), sem("w_evac_dve")
        w_mul, w_acc = sem("w_mul"), sem("w_acc")
        stack_in = [sem(f"stack_in{u}") for u in range(3)]
        max_in = [sem(f"max_in{T}") for T in range(2)]
        scratch = [sem(f"scratch{u}") for u in range(3)]
        nat_ready, nat_used = sem("nat_ready"), sem("nat_used")
        max_neg, max_split = sem("max_neg"), sem("max_split")
        max_turned, max_rows = sem("max_turned"), sem("max_rows")
        st_ready, exp_done, mask_done, prob_used = (sem("st_ready"), sem("exp_done"),
                                                    sem("mask_done"), sem("prob_used"))
        pv_copied = sem("pv_copied")
        ctx_turned, den_ready, ctx_ready = sem("ctx_turned"), sem("den_ready"), sem("ctx_ready")
        split_act, split_pool = sem("split_act"), sem("split_pool")
        q_turned, q_rows = sem("q_turned"), sem("q_rows")
        ctx_in = sem("ctx_in")
        h1_ready, fin_ready = sem("h1_ready"), sem("fin_ready")
        e_job, e_act, e_dve = sem("e_job"), sem("e_act"), sem("e_dve")
        e_var, e_std = sem("e_var"), sem("e_std")
        e_hn = sem("e_hn")
        pool_tally, pe_tally = sem("pool_tally"), sem("pe_tally")
        stored = [sem(f"stored{r}") for r in range(4)]

        jobs = [("wqkv", kc, half) for kc in range(2) for half in range(2)] + [("wo", 0, 0)]
        jobs += [("turn", 0, 0), ("turn", 1, 0)]
        for n in range(4):
            if n < 3:
                jobs += [("turn", 2 * n + 2, 0), ("turn", 2 * n + 3, 0)]
            jobs += [("qk", m, n) for m in range(4)]
            jobs += [("v", 2 * n, 0), ("v", 2 * n + 1, 0)]
        RING = 6
        by_dve = [j[0] in ("qk", "v") for j in jobs]

        def copied(e, k):
            if by_dve[k]:
                e.wait_ge(job_dve, sum(by_dve[:k + 1]))
            else:
                e.wait_ge(job_act, k + 1 - sum(by_dve[:k + 1]))

        block = ctx.enter_context(nc.Block())

        @block.sync
        def _(sp):
            sp.dma_start(idx_row[:], x.rearrange("b (k p) -> (b k) p", p=P)).then_inc(in_x, 16)
            sp.dma_start(bias_row[:], bqkv[0:2 * D].rearrange("(m p) -> m p", p=P)).then_inc(in_x, 16)
            for m in range(4):
                for g in range(2):
                    row = m * P + g * GW
                    sp.dma_start(wn[g * GW:(g + 1) * GW, m, :],
                                 wqkv[row:row + GW, :].rearrange("(h d) c -> d h c", h=HG)).then_inc(in_w, 16)
            sp.dma_start(wn[:, 4:6, :], wqkv[2 * D:3 * D, :].rearrange("(m p) c -> p m c", p=P)).then_inc(in_w, 16)
            sp.dma_start(own[:], out_w.rearrange("(m p) c -> p m c", p=P)).then_inc(in_w, 16)
            sp.dma_start(bias_v[:], bqkv[2 * D:3 * D].partition_broadcast(P)).then_inc(in_b, 16)
            sp.dma_start(bias_o[:], out_b.partition_broadcast(P)).then_inc(in_b, 16)

            writes = 0
            for n in range(4):
                b, half = n // 2, n % 2
                for m in range(4):
                    x_n = 4 * n + m
                    sp.wait_ge(x_lo, x_n + 1)
                    for g in range(2):
                        at = GROUPS * b + 2 * (m % 2) + g
                        dst = q_d[at, :, half] if m < 2 else k_d[at, :, :, 512 * half:512 * half + 512]
                        sp.dma_start(dst.rearrange("a r t -> r a t"),
                                     parts[x_n % 4][g * GW:(g + 1) * GW]).then_inc(part_out[x_n % 4], 16)
                for k in range(4 * n, 4 * n + 4):
                    sp.wait_ge(job_dve, 6 * n + 4 + (k - 4 * n) // 2 + 1)
                    dst = v_d[GROUPS * b:GROUPS * (b + 1), :, k % TB, :].rearrange("g s f -> s g f")
                    sp.dma_start(dst, vt[:, k % 4].rearrange("p g h o d -> p g (h o d)")).then_inc(vt_out[k % 4], 16)
            for r in range(4):
                sp.wait_ge(part_out[r], 16 * 8)
                sp.wait_ge(vt_out[r], 16 * 4)

            def load(s):
                at = s.n % BG
                for k, (pq, pk) in enumerate(zip(PIECES_Q, PIECES_K)):
                    rows = slice(k * HD, (k + 1) * HD)
                    sp.dma_start(qst[rows, s.u, :].rearrange("p (T c) -> p T c", T=2), q_d[at, pq].rearrange("T (d h) t -> d T (h t)", h=HG)).then_inc(stack_in[s.u], 16)
                    sp.dma_start(kst[rows, s.u, :], k_d[at, pk].rearrange("(d h) t -> d (h t)", h=HG)).then_inc(stack_in[s.u], 16)
                sp.dma_start(vst[:, s.u].rearrange("p j h d -> p (j h d)"),
                             v_d[at].rearrange("s j f -> s (j f)")).then_inc(stack_in[s.u], 16)

            def max_to_stack(s, T):
                sp.wait_ge(max_rows, 2 * s.n + T + 1)
                for a in range(3):
                    dst = qst[KS + a:KS + a + 1, s.u, 2048 * T:2048 * (T + 1)].rearrange("p (r t) -> p r t", t=P)
                    sp.dma_start(dst, mrow[16 * a:16 * a + 16, T, :]).then_inc(max_in[T], 16)

            def context_out(s):
                sp.wait_ge(ctx_ready, 2 * s.n + 2)
                sp.dma_start(c_d[s.n % BG], cn[:].rearrange("p j d h -> p (j d h)")).then_inc(scratch[s.u], 16)

            def step(s, has_ctx, has_next, has_load):
                max_to_stack(s, 1)
                if has_load:
                    if has_ctx:
                        sp.wait_ge(prob_used, NQ * s.n)
                        sp.wait_ge(scratch[s.u], WBASE + 16 * CWRITES * (s.q - 1))
                    load(s.add(2))
                if has_ctx:
                    c = s.add(-1)
                    sp.wait_ge(scratch[c.u], WBASE + 16 * CWRITES * c.q)
                    context_out(c)
                    at = c.n % BG
                    sp.wait_ge(q_rows, 2 * c.n + 1)
                    for a in range(2):
                        sp.dma_start(q_d[at, a].rearrange("T r t -> r T t"),
                                     qT1[a * GW:(a + 1) * GW, :].rearrange("r (T t) -> r T t", T=2)).then_inc(scratch[c.u], 16)
                    sp.wait_ge(q_rows, 2 * c.n + 2)
                    sp.dma_start(q_d[at, 2].rearrange("T r t -> r T t"),
                                 qT2[:].rearrange("r (T t) -> r T t", T=2)).then_inc(scratch[c.u], 16)
                if has_next:
                    max_to_stack(s.add(1), 0)

            for u in range(3):
                sp.sem_inc(scratch[u], WBASE)
            load(Step(0, 0))
            load(Step(0, 1))
            max_to_stack(Step(0, 0), 0)
            over_steps(sp, step)

            last = Step(0, STEPS - 1)
            context_out(last)
            sp.wait_ge(scratch[0], WBASE + 16 * CWRITES * 8)
            sp.wait_ge(scratch[1], WBASE + 16 * CWRITES * 8)
            sp.wait_ge(scratch[2], WBASE + 16 * CWRITES * 7 + 16)
            sp.wait_ge(prob_used, NQ * STEPS)
            for at in range(BG):
                b, g = at // GROUPS, at % GROUPS
                sp.dma_start(cx[:, TB * b:TB * (b + 1), GW * g:GW * (g + 1)],
                             c_d[at].rearrange("p (j c) -> p j c", j=TB)).then_inc(ctx_in, 16)
            for k in range(NT):
                sp.wait_ge(fin_ready, k + 1)
                sp.dma_start(out.rearrange("b (j p) d -> p (b j) d", p=P)[:, k, :],
                             res[:, k % 4, :]).then_inc(stored[k % 4], 16)
            for r in range(4):
                sp.wait_ge(stored[r], 16 * NT // 4)

        @block.gpsimd
        def _(pool):
            count = [0]

            def link(ins, more=None):
                count[0] += 1
                ins.then_inc(pchain, 1)
                pool.wait_ge(pchain, count[0])

            link(pool.memset(identf[:], 0.0))
            pool.affine_select(out=identf[:], in_=identf[:], compare_op=ALU.not_equal, fill=1.0,
                               base=0, pattern=[[-1, P]], channel_multiplier=1).then_inc(consts, 1)
            pool.wait_ge(consts, 1)
            pool.tensor_copy(identb[:], identf[:]).then_inc(consts, 1)
            link(pool.memset(mask_l[:], 0.0))
            pool.affine_select(out=mask_l[:], in_=mask_l[:], compare_op=ALU.not_equal, fill=125.0,
                               base=0, pattern=[[-1, P]], channel_multiplier=1).then_inc(consts, 1)
            link(pool.memset(mask_r[:], 0.0))
            pool.affine_select(out=mask_r[:], in_=mask_r[:], compare_op=ALU.is_ge, fill=NEG / 125.0,
                               base=0, pattern=[[-1, P]], channel_multiplier=1).then_inc(consts, 1)
            pool.memset(vt[:], 1.0).then_inc(consts, 1)
            pool.wait_ge(idx_ready, 1)
            for k in range(NT):
                pool.indirect_dma_start(
                    out=h[:, k, :], out_offset=None, in_=tok_w,
                    in_offset=bass.IndirectOffsetOnAxis(ap=idx[:, k:k + 1], axis=0)).then_inc(gathered[k // 4], 16)

            def load_w(e, r):
                pool.dma_start(w1b[:, r], w1[e].rearrange("(k p) n -> p k n", p=P)).then_inc(w_loaded[r], 16)
                pool.dma_start(w2b[:, r], w2[e].rearrange("(k p) n -> p k n", p=P)).then_inc(w_loaded[r], 16)

            load_w(0, 0)
            load_w(1, 1)
            pool.wait_ge(consts, 5)
            for u in range(2):
                pool.memset(kst[KS:KM, u, :], 1.0).then_inc(ones_set, 1)
                pool.wait_ge(ones_set, u + 1)
            for r in range(4):
                pool.wait_ge(part_out[r], 16 * 8)
            pool.memset(kst[KS:KM, 2, :], 1.0).then_inc(ones_set, 1)
            pool.wait_ge(ones_set, 3)
            with pool.Fori(1, NEXP // 2) as i:
                for r in range(2):
                    pool.wait_ge(w_mul, 2 * i + r - 1)
                    load_w(2 * i + r, r)

            def split_max(s, T):
                done = 8 * s.n + 4 * T
                wait_alone(pool, max_neg, 2 * s.n + T + 1, pool_tally)
                if not (isinstance(s.n, int) and s.n == 0):
                    wait_alone(pool, max_turned, 2 * s.n + T - 1, pool_tally)
                pool.tensor_copy(msp[:, T, 0, :], negm[:, T]).then_inc(max_split, 1)
                wait_alone(pool, max_split, done + 1, pool_tally)
                pool.tensor_tensor(mrest[:, T], negm[:, T], msp[:, T, 0, :], ALU.subtract).then_inc(max_split, 1)
                wait_alone(pool, max_split, done + 2, pool_tally)
                pool.tensor_copy(msp[:, T, 1, :], mrest[:, T]).then_inc(max_split, 1)
                wait_alone(pool, max_split, done + 3, pool_tally)
                pool.tensor_tensor(msp[:, T, 2, :], mrest[:, T], msp[:, T, 1, :], ALU.subtract).then_inc(max_split, 1)

            def step(s, has_ctx, has_next, has_load):
                c = s.add(-1)
                for what, *at in PLAN:
                    if what == "parts" and has_next:
                        split_max(s.add(1), at[0])
                    if what == "st" and QUADS[at[0]][4]:
                        qd, ci = at
                        chunks, pitch = head_chunks(QUADS[qd][2])
                        wait_alone(pool, exp_done, NC * s.n + CHUNKS_TO[qd] + ci + 1, pool_tally)
                        v = prob[:, qd % 3, 1024 * ci:1024 * ci + pitch * len(chunks[ci])]
                        v = v.rearrange("p (h c) -> p h c", c=pitch)[:, :, 0:P]
                        pool.affine_select(out=v, in_=v, compare_op=ALU.is_ge, fill=0.0, base=0,
                                           pattern=[[0, len(chunks[ci])], [1, P]],
                                           channel_multiplier=-1).then_inc(mask_done, 1)
                    if what == "rest" and has_ctx:
                        wait_alone(pool, split_act, 2 * c.n + 1, pool_tally)
                        pool.tensor_tensor(crest[:], cn[:].rearrange("p j d h -> p j (d h)"), qn[:, :, 0, :],
                                           ALU.subtract).then_inc(split_pool, 1)
                    if what == "low" and has_ctx:
                        wait_alone(pool, split_act, 2 * c.n + 2, pool_tally)
                        pool.tensor_tensor(qn[:, :, 2, :], crest[:], qn[:, :, 1, :], ALU.subtract).then_inc(split_pool, 1)

            split_max(Step(0, 0), 0)
            split_max(Step(0, 0), 1)
            over_steps(pool, step)

        @block.scalar
        def _(act):
            def make_mid(x_n):
                act.wait_ge(x_rest, x_n + 1)
                act.copy(parts[x_n % 4][:, 1, :], rs[:, x_n % 3, :]).then_inc(x_mid, 1)

            x_n = 0
            for k, (kind, a, c) in enumerate(jobs):
                if kind == "turn" and a % 2 == 0:
                    act.wait_ge(var_ready, a // 2 + 1)
                    act.activation(std[:, 2 * a:2 * a + 4], var[:, 2 * a:2 * a + 4],
                                   ACT.Sqrt).then_inc(std_ready, 1)
                if not by_dve[k]:
                    act.wait_ge(job_done, k + 1)
                    bank = ps[:, k % RING, :]
                    if kind == "wqkv":
                        w = 512 if c == 0 else 256
                        act.copy(wT[:, a, 512 * c:512 * c + w], bank[:, 0:w]).then_inc(job_act, 1)
                    elif kind == "wo":
                        act.copy(woT[:].rearrange("p k n -> p (k n)"), bank).then_inc(job_act, 1)
                    else:
                        act.copy(xT[:, :, 256 * a:256 * a + 256],
                                 bank.rearrange("p (k n) -> p k n", k=2)).then_inc(job_act, 1)
                if kind == "qk":
                    act.wait_ge(job_dve, sum(by_dve[:k + 1]))
                    if x_n >= 4:
                        act.wait_ge(part_out[x_n % 4], 32 * (x_n // 4))
                    act.copy(parts[x_n % 4][:, 0, :], xs[:, x_n % 3, :]).then_inc(x_hi, 1)
                    if a >= 1:
                        make_mid(x_n - 1)
                    x_n += 1
                if kind == "v" and a % 2 == 0:
                    make_mid(x_n - 1)

            def w_copies(e):
                act.wait_ge(w_turned, e + 1)
                for k in range(2):
                    act.copy(w1T[:, 4 * k:4 * k + 2, :].rearrange("p a n -> p (a n)"),
                             ps[:, 2 * k, :]).then_inc(w_evac_act, 1)

            with act.Fori(0, NEXP) as e:
                w_copies(e)

            def copy_context(s, T):
                act.wait_ge(prob_used, NQ * s.n + (4 if T == 0 else NQ))
                act.copy(cT[:, T, :], ps[:, PV_BANK, :]).then_inc(pv_copied, 1)

            def copy_max(s, T):
                act.wait_ge(max_turned, 2 * s.n + T + 1)
                if not (isinstance(s.n, int) and s.n == 0):
                    act.wait_ge(max_in[T], 48 * s.n)
                act.copy(mrow[:, T, :], misc_bf[0:48, 0:P]).then_inc(max_rows, 1)

            def exps(s, qd, ci):
                w = QUADS[qd][2]
                chunks, pitch = head_chunks(w)
                if ci == 0 and not (isinstance(s.n, int) and NQ * s.n + qd < 3):
                    act.wait_ge(prob_used, NQ * s.n + qd - 2)
                ch, n = CHUNKS_TO[qd] + ci, len(chunks[ci])
                act.wait_ge(st_ready, NC * s.n + ch + 1)
                src = ps[:, ST_BANK + 2 * (ch % 2):ST_BANK + 2 * (ch % 2) + 2, :].rearrange("p a c -> p (a c)")
                src = src[:, 0:n * pitch].rearrange("p (h c) -> p h c", c=pitch)[:, :, 0:w]
                dst = prob[:, qd % 3, 1024 * ci:1024 * ci + n * pitch]
                dst = dst.rearrange("p (h c) -> p h c", c=pitch)[:, :, 0:w]
                act.activation(dst, src, ACT.Exp).then_inc(exp_done, 1)

            def step(s, has_ctx, has_next, has_load):
                c = s.add(-1)
                for what, *at in PLAN:
                    if what == "st":
                        exps(s, *at)
                    if what == "copy" and (at[0] == 0 or has_ctx):
                        copy_context(s if at[0] == 0 else c, at[0])
                    if what == "hi" and has_ctx:
                        act.wait_ge(ctx_ready, 2 * c.n + 2)
                        act.copy(qn[:, :, 0, :], cn[:].rearrange("p j d h -> p j (d h)")).then_inc(split_act, 1)
                    if what == "mid" and has_ctx:
                        act.wait_ge(split_pool, 2 * c.n + 1)
                        act.copy(qn[:, :, 1, :], crest[:]).then_inc(split_act, 1)
                    if what == "qt" and has_ctx:
                        act.wait_ge(q_turned, 2 * s.n - 1 + at[0])
                        if at[0] == 0:
                            act.copy(qT1[:], misc_bf).then_inc(q_rows, 1)
                        else:
                            act.copy(qT2[:], misc_bf[0:GW, :]).then_inc(q_rows, 1)
                    if what == "max" and at[0] == 0 and has_next:
                        copy_max(s.add(1), 0)
                    if what == "max" and at[0] == 1:
                        copy_max(s, 1)

            copy_max(Step(0, 0), 0)
            over_steps(act, step)
            copy_context(Step(0, STEPS - 1), 1)

            for k in range(8):
                act.wait_ge(e_job, k + 1)
                act.copy(xT[:, :, 256 * k:256 * k + 256],
                         ps[:, k % 2, :].rearrange("p (k n) -> p k n", k=2)).then_inc(e_act, 1)
            for n in range(4):
                act.wait_ge(e_var, n + 1)
                act.activation(std[:, 4 * n:4 * n + 4], var[:, 4 * n:4 * n + 4], ACT.Sqrt).then_inc(e_std, 1)
                for k in (8 + 2 * n, 9 + 2 * n):
                    act.wait_ge(e_job, k + 1)
                    act.copy(xT[:, :, 256 * (k - 8):256 * (k - 8) + 256],
                             ps[:, k % 2, :].rearrange("p (k n) -> p k n", k=2)).then_inc(e_act, 1)

        @block.vector
        def _(dve):
            count = [0]

            def link(ins):
                count[0] += 1
                ins.then_inc(dchain, 1)
                dve.wait_ge(dchain, count[0])

            def norm_stats(n, ready):
                for k in range(4 * n, 4 * n + 4):
                    last = dve.bn_stats(stats[:, k, :], h[:, k, :])
                link(last)
                for k in range(4 * n, 4 * n + 4):
                    last = dve.bn_aggr(mv[:, k, :], stats[:, k, :])
                link(last)
                dve.tensor_scalar_add(var[:, 4 * n:4 * n + 4], mv[:, 4 * n:4 * n + 4, 1], EPS).then_inc(ready, 1)

            def normalise(n, root, dst):
                dve.wait_ge(root, n + 1)
                link(dve.reciprocal(rstd[:, 4 * n:4 * n + 4], std[:, 4 * n:4 * n + 4]))
                for k in range(4 * n, 4 * n + 4):
                    last = dve.tensor_scalar(dst[:, k % dst.shape[1], :], h[:, k, :], mv[:, k, 0:1], rstd[:, k:k + 1],
                                             ALU.subtract, ALU.mult)
                return last

            dve.wait_ge(in_x, 32)
            dve.tensor_copy(idx_f[:], idx_row[:]).then_inc(rows_ready, 1)
            dve.tensor_copy(bias_p[:].rearrange("m (g d h) -> m g d h", d=HD, h=HG),
                            bias_row[:].rearrange("m (g h d) -> m g d h", h=HG, d=HD)).then_inc(rows_ready, 1)
            dve.wait_ge(rows_turned, 1)
            dve.tensor_copy(idx[:], misc[:, 0:NT]).then_inc(idx_ready, 1)
            link(dve.tensor_copy(bias_qk[:], misc[:, NT:NT + 4]))
            link(dve.memset(w12[:], 0.0))
            link(dve.memset(mx[:], ROW_LOW))
            dve.wait_ge(in_w, 16 * 10)
            for o in range(2):
                last = dve.tensor_copy(owp[:, o, :].rearrange("p (g d h) -> p g d h", d=HD, h=HG),
                                       own[:, o, :].rearrange("p (g h d) -> p g d h", d=HD, h=HG))
            last.then_inc(owp_ready, 1)
            dve.wait_ge(in_b, 16 * 2)

            def make_rest(x_n):
                dve.wait_ge(x_hi, x_n + 1)
                dve.tensor_tensor(rs[:, x_n % 3, :], xs[:, x_n % 3, :], parts[x_n % 4][:, 0, :],
                                  ALU.subtract).then_inc(x_rest, 1)

            def make_low(x_n):
                dve.wait_ge(x_mid, x_n + 1)
                dve.tensor_tensor(parts[x_n % 4][:, 2, :], rs[:, x_n % 3, :], parts[x_n % 4][:, 1, :],
                                  ALU.subtract).then_inc(x_lo, 1)

            x_n = 0
            for k, (kind, a, c) in enumerate(jobs):
                if kind == "turn" and a % 2 == 0:
                    n = a // 2
                    dve.wait_ge(gathered[n], 64)
                    norm_stats(n, var_ready)
                    if n >= 1:
                        dve.wait_ge(job_done, jobs.index(("turn", 2 * n - 1, 0)) + 1)
                    normalise(n, std_ready, hn).then_inc(hn_ready, 1)
                if kind == "qk":
                    dve.wait_ge(job_done, k + 1)
                    scale = 1.0 if a < 2 else KEY_SCALE
                    dve.tensor_scalar(xs[:, x_n % 3, :], ps[:, k % RING, :], bias_qk[:, a:a + 1], scale,
                                      ALU.add, ALU.mult).then_inc(job_dve, 1)
                    if a >= 1:
                        make_rest(x_n - 1)
                    if a >= 2:
                        make_low(x_n - 2)
                    x_n += 1
                if kind == "v":
                    if a % 2 == 0:
                        make_rest(x_n - 1)
                        make_low(x_n - 2)
                    else:
                        make_low(x_n - 1)
                    dve.wait_ge(job_done, k + 1)
                    for r in range(2):
                        blk = 2 * a + r
                        if blk < 4:
                            dve.wait_ge(consts, 5)
                        else:
                            dve.wait_ge(vt_out[blk % 4], 16 * (blk // 4))
                        last = dve.tensor_tensor(
                            vt[:, blk % 4, :, :, 0, :],
                            ps[:, k % RING, 256 * r:256 * r + 256].rearrange("p (g h d) -> p g h d", g=GROUPS, h=HG),
                            bias_v[:].rearrange("p (g h d) -> p g h d", g=GROUPS, h=HG), ALU.add)
                    last.then_inc(job_dve, 1)
            for k in range(NT):
                last = dve.tensor_tensor(h[:, k, :], h[:, k, :], bias_o[:], ALU.add)
            link(last)

            with dve.Fori(0, NEXP) as e:
                dve.wait_ge(w_turned, e + 1)
                for k in range(2):
                    dve.tensor_copy(w1T[:, 4 * k + 2:4 * k + 4, :].rearrange("p a n -> p (a n)"),
                                    ps[:, 2 * k + 1, :]).then_inc(w_evac_dve, 1)
                dve.wait_ge(w_mul, e + 1)
                dve.tensor_tensor(w12[:], w12[:], ps[:, 4:6, 0:D], ALU.add).then_inc(w_acc, 1)

            def row_max(s, c):
                i, half, heads, k0, w, diag = NAT[c]
                dve.wait_ge(nat_ready, NN * s.n + c + 1)
                if c == 0 and not (isinstance(s.n, int) and s.n == 0):
                    dve.wait_ge(max_neg, 2 * s.n)
                src = ps[:, NAT_BANK + c % 2, 0:w * len(heads)].rearrange("p (h c) -> p h c", c=w)
                dve.tensor_reduce(mx[:, heads[0]:heads[-1] + 1, i, half], src, AX.X, ALU.max).then_inc(nat_used, 1)

            def finish_max(s, T):
                dve.wait_ge(nat_used, NN * s.n + (NN if T else NAT_HALF))
                if not (isinstance(s.n, int) and s.n == 0):
                    dve.wait_ge(max_split, 8 * s.n + 4 * T - 4)
                dve.tensor_reduce(negm[:, T].rearrange("p (h i) -> p h i", h=HG), mx[:, :, 4 * T:4 * T + 4, :],
                                  AX.X, ALU.max, negate=True).then_inc(max_neg, 1)

            def divide(s, T):
                dve.wait_ge(ctx_turned, 2 * s.n + T + 1)
                tile = misc.rearrange("p (j h c) -> p j h c", j=4, h=HG)
                dve.reciprocal(rden[:].rearrange("p (j h) -> p j h", j=4), tile[:, :, :, HD]).then_inc(den_ready, 1)
                dve.wait_ge(den_ready, 2 * s.n + T + 1)
                if T == 0 and not (isinstance(s.n, int) and s.n == 0):
                    p = s.add(-1)
                    dve.wait_ge(scratch[p.u], WBASE + 16 * CWRITES * (p.q + 1))
                dve.tensor_tensor(
                    cn[:, 4 * T:4 * T + 4].rearrange("p j d h -> p j h d"), tile[:, :, :, 0:HD],
                    rden[:].rearrange("p (j h) -> p j h", j=4).unsqueeze(3).broadcast_to([P, 4, HG, HD]),
                    ALU.mult).then_inc(ctx_ready, 1)

            def step(s, has_ctx, has_next, has_load):
                for what, *at in PLAN:
                    if what == "nat" and has_next:
                        row_max(s.add(1), at[0])
                        if at[0] in (NAT_HALF - 1, NN - 1):
                            finish_max(s.add(1), at[0] // (NN - 1))
                    if what == "ctx" and has_ctx:
                        divide(s.add(-1), at[0])

            for c in range(NN):
                row_max(Step(0, 0), c)
                if c in (NAT_HALF - 1, NN - 1):
                    finish_max(Step(0, 0), c // (NN - 1))
            over_steps(dve, step)
            for T in range(2):
                divide(Step(0, STEPS - 1), T)

            for n in range(4):
                for k in range(4 * n, 4 * n + 4):
                    dve.wait_ge(h1_ready, k + 1)
                    last = dve.tensor_tensor(h[:, k, :], h[:, k, :], ps[:, 2 + k % 2, 0:D], ALU.add)
                    last.then_inc(e_dve, 1)
                dve.wait_ge(e_dve, 4 * n + 4)
                norm_stats(n, e_var)
                normalise(n, e_std, hn2).then_inc(e_hn, 1)
            for k in range(NT):
                dve.wait_ge(h1_ready, NT + k + 1)
                if k >= 4:
                    dve.wait_ge(stored[k % 4], 16 * (k // 4))
                dve.tensor_tensor(res[:, k % 4, :], h[:, k, :], ps[:, 2 + k % 2, 0:D], ALU.add).then_inc(fin_ready, 1)

        @block.tensor
        def _(pe):
            pe.wait_ge(consts, 1)
            pe.wait_ge(rows_ready, 2)
            pe.transpose(misc[:, 0:NT], idx_f[:], identf[0:NT, 0:NT])
            pe.transpose(misc[:, NT:NT + 4], bias_p[:], identf[0:4, 0:4]).then_inc(rows_turned, 1)
            for k, (kind, a, c) in enumerate(jobs):
                if k >= RING:
                    copied(pe, k - RING)
                bank = ps[:, k % RING, :]
                if kind == "wqkv":
                    pe.wait_ge(in_w, 16 * 10)
                    for x_m, m in enumerate(range(4 * c, 4 * c + (4 if c == 0 else 2))):
                        last = pe.transpose(bank[:, x_m * P:(x_m + 1) * P], wn[:, m, a * P:(a + 1) * P], identf[:])
                elif kind == "wo":
                    pe.wait_ge(owp_ready, 1)
                    for kc in range(2):
                        for o in range(2):
                            last = pe.transpose(bank[:, (2 * kc + o) * P:(2 * kc + o + 1) * P],
                                                owp[:, o, kc * P:(kc + 1) * P], identf[:])
                elif kind == "turn":
                    pe.wait_ge(hn_ready, a // 2 + 1)
                    for kc in range(2):
                        for r in range(2):
                            last = pe.transpose(bank[:, 256 * kc + P * r:256 * kc + P * (r + 1)],
                                                hn[:, (2 * a + r) % 4, kc * P:(kc + 1) * P], identf[:])
                elif kind == "qk":
                    copied(pe, max(j for j in range(k) if jobs[j][0] == "turn" and jobs[j][1] <= 2 * c + 1))
                    for kc in range(2):
                        last = pe.matmul(bank, wT[:, kc, a * P:(a + 1) * P], xT[:, kc, 512 * c:512 * c + 512],
                                         start=(kc == 0), stop=(kc == 1))
                else:
                    for r in range(2):
                        blk = 2 * a + r
                        for kc in range(2):
                            last = pe.matmul(bank[:, 256 * r:256 * r + 256], xT[:, kc, blk * P:(blk + 1) * P],
                                             wT[:, kc, 2 * D:3 * D], start=(kc == 0), stop=(kc == 1))
                last.then_inc(job_done, 1)

            for k in range(len(jobs) - RING, len(jobs)):
                copied(pe, k)

            def turn_w(e, r, uses):
                pe.wait_ge(w_loaded[r], 32 * uses)
                for k in range(8):
                    for kc in range(2):
                        last = pe.transpose(ps[:, k // 2, 256 * (k % 2) + P * kc:256 * (k % 2) + P * (kc + 1)],
                                            w1b[:, r, kc, P * k:P * (k + 1)], identf[:])
                last.then_inc(w_turned, 1)

            def mul_w(e, r):
                pe.wait_ge(w_evac_act, 2 * e + 2)
                pe.wait_ge(w_evac_dve, 2 * e + 2)
                for m in range(2):
                    for k in range(8):
                        last = pe.matmul(ps[:, 4 + m, 0:D], w1T[:, k, m * P:(m + 1) * P], w2b[:, r, k, :],
                                         start=(k == 0), stop=(k == 7))
                last.then_inc(w_mul, 1)

            with pe.Fori(0, NEXP // 2) as i:
                for r in range(2):
                    turn_w(2 * i + r, r, i + 1)
                    mul_w(2 * i + r, r)
                    pe.wait_ge(w_acc, 2 * i + r + 1)

            def row_scores(s, c):
                i, half, heads, k0, w, diag = NAT[c]
                if not (isinstance(s.n, int) and NN * s.n + c < 2):
                    pe.wait_ge(nat_used, NN * s.n + c - 1)
                for x_h, a in enumerate(heads):
                    q0 = 2048 * (i // 4) + 512 * a + P * (i % 4)
                    o = ps[:, NAT_BANK + c % 2, x_h * w:(x_h + 1) * w]
                    last = pe.matmul(o, qst[0:KS, s.u, q0:q0 + P],
                                     kst[0:KS, s.u, S * a + k0:S * a + k0 + w], start=True, stop=not diag)
                    if diag:
                        last = pe.matmul(o[:, w - P:w], mask_l[:], mask_r[:], start=False, stop=True)
                last.then_inc(nat_ready, 1)

            def key_scores(s, qd, ci):
                T, j, w, off, diag = QUADS[qd]
                chunks, pitch = head_chunks(w)
                ch = CHUNKS_TO[qd] + ci
                if j == 0 and ci == 0:
                    pe.wait_ge(max_in[T], 48 * (s.n + 1))
                if not (isinstance(s.n, int) and NC * s.n + ch < 2):
                    pe.wait_ge(exp_done, NC * s.n + ch - 1)
                slot = ps[:, ST_BANK + 2 * (ch % 2):ST_BANK + 2 * (ch % 2) + 2, :].rearrange("p a c -> p (a c)")
                for x_h, a in enumerate(chunks[ci]):
                    t0 = 2048 * T + 512 * a + off
                    last = pe.matmul(slot[:, x_h * pitch:x_h * pitch + w],
                                     kst[0:KM, s.u, S * a + P * j:S * a + P * (j + 1)],
                                     qst[0:KM, s.u, t0:t0 + w], start=True, stop=True)
                last.then_inc(st_ready, 1)

            def values(s, qd):
                T, j, w, off, diag = QUADS[qd]
                chunks, pitch = head_chunks(w)
                pe.wait_ge(exp_done, NC * s.n + CHUNKS_TO[qd + 1])
                if diag:
                    pe.wait_ge(mask_done, NM * s.n + MASKS_TO[qd + 1])
                if j == 0 and not (isinstance(s.n, int) and 2 * s.n + T == 0):
                    pe.wait_ge(pv_copied, 2 * s.n + T)
                for ci, heads in enumerate(chunks):
                    for x_h, a in enumerate(heads):
                        c0 = 1024 * ci + x_h * pitch
                        last = pe.matmul(ps[32 * a:32 * a + 32, PV_BANK, off:off + w], vst[:, s.u, j, a, :],
                                         prob[:, qd % 3, c0:c0 + w], start=(j == 0), stop=(j == 4 * T + 3))
                last.then_inc(prob_used, 1)

            def turn_max(s, T):
                wait_alone(pe, max_split, 8 * s.n + 4 * T + 4, pe_tally)
                pe.transpose(misc_bf[0:48, 0:P], msp[:, T].rearrange("p a r -> p (a r)"), identb[:]).then_inc(max_turned, 1)

            def turn_context(s, T):
                pe.wait_ge(pv_copied, 2 * s.n + T + 1)
                if T == 0 and isinstance(s.n, int) and s.n == STEPS - 1:
                    pe.wait_ge(q_rows, 2 * s.n)
                elif T == 0:
                    pe.wait_ge(max_rows, 2 * s.n + 4)
                else:
                    pe.wait_ge(ctx_ready, 2 * s.n + 1)
                for j in range(4):
                    last = pe.transpose(misc[:, P * j:P * (j + 1)], cT[:, T, P * j:P * (j + 1)], identf[:])
                last.then_inc(ctx_turned, 1)

            def turn_queries(s, half):
                if half == 0:
                    pe.wait_ge(split_pool, 2 * s.n + 2)
                else:
                    wait_alone(pe, q_rows, 2 * s.n + 1, pe_tally)
                cols = slice(0, P) if half == 0 else slice(P, P + GW)
                rows = P if half == 0 else GW
                for j in range(TB):
                    last = pe.transpose(misc_bf[0:rows, P * j:P * (j + 1)],
                                        qn[:, j].rearrange("p a r -> p (a r)")[:, cols], identb[:])
                last.then_inc(q_turned, 1)

            def step(s, has_ctx, has_next, has_load):
                nxt, c = s.add(1), s.add(-1)
                for what, *at in PLAN:
                    if what == "nat" and has_next:
                        if at[0] == 0:
                            pe.wait_ge(stack_in[nxt.u], 16 * LOADS * (nxt.q + 1))
                        row_scores(nxt, at[0])
                    if what == "st":
                        key_scores(s, *at)
                    if what == "pv" and (at[0] >= 0 or has_ctx):
                        values(*((s, at[0]) if at[0] >= 0 else (c, NQ + at[0])))
                    if what == "ctx" and has_ctx:
                        turn_context(c, at[0])
                    if what == "qt" and has_ctx:
                        turn_queries(c, at[0])
                    if what == "max" and at[0] == 0 and has_next:
                        if has_ctx:
                            pe.wait_ge(q_rows, 2 * s.n)
                        else:
                            pe.wait_ge(max_rows, 2)
                        turn_max(nxt, 0)
                    if what == "max" and at[0] == 1:
                        pe.wait_ge(max_rows, 2 * s.n + 1)
                        turn_max(s, 1)

            pe.wait_ge(consts, 5)
            pe.wait_ge(stack_in[0], 16 * LOADS)
            for c in range(NN):
                row_scores(Step(0, 0), c)
            turn_max(Step(0, 0), 0)
            pe.wait_ge(ones_set, 3)
            over_steps(pe, step)
            last_step = Step(0, STEPS - 1)
            values(last_step, NQ - 2)
            values(last_step, NQ - 1)
            for T in range(2):
                turn_context(last_step, T)

            pe.wait_ge(ctx_in, 16 * BG)
            for k in range(8):
                if k >= 2:
                    pe.wait_ge(e_act, k - 1)
                for kc in range(2):
                    for r in range(2):
                        blk = 2 * k + r
                        last = pe.transpose(ps[:, k % 2, 256 * kc + P * r:256 * kc + P * (r + 1)],
                                            cx[:, blk, kc * P:(kc + 1) * P], identf[:])
                last.then_inc(e_job, 1)

            def product(k, w, turned):
                pe.wait_ge(e_act, turned)
                for kc in range(2):
                    last = pe.matmul(ps[:, 2 + k % 2, 0:D], xT[:, kc, k * P:(k + 1) * P], w[:, kc, :],
                                     start=(kc == 0), stop=(kc == 1))
                last.then_inc(h1_ready, 1)

            def turn_norm(n):
                pe.wait_ge(e_hn, n + 1)
                for k in (2 * n, 2 * n + 1):
                    pe.wait_ge(e_act, 8 + k - 1)
                    for kc in range(2):
                        for r in range(2):
                            last = pe.transpose(ps[:, k % 2, 256 * kc + P * r:256 * kc + P * (r + 1)],
                                                hn2[:, 2 * k + r, kc * P:(kc + 1) * P], identf[:])
                    last.then_inc(e_job, 1)

            for n in range(4):
                for k in range(4 * n, 4 * n + 4):
                    if k >= 2:
                        pe.wait_ge(e_dve, k - 1)
                    product(k, woT, k // 2 + 1)
                if n >= 1:
                    turn_norm(n - 1)
            turn_norm(3)
            for k in range(NT):
                if k >= 2:
                    pe.wait_ge(fin_ready, k - 1)
                else:
                    pe.wait_ge(e_dve, NT)
                product(k, w12, 8 + k // 2 + 1)


def kernel(**inputs):
    import numpy as np
    import concourse.bacc as bacc
    from concourse.bass_utils import run_bass_kernel_spmd

    nc = bacc.Bacc("TRN2", target_bir_lowering=False, num_devices=1)
    names = ["x", "L0_tok_W", "L0_attn_Wqkv_w", "L0_attn_Wqkv_b", "L0_attn_out_w", "L0_attn_out_b",
             "L0_ffn_w1", "L0_ffn_w2"]
    arrays, args = {}, []
    for name in names:
        a = np.ascontiguousarray(inputs[name])
        arrays[f"in_{name}"] = a
        args.append(nc.dram_tensor(f"in_{name}", a.shape, mybir.dt.from_np(a.dtype), kind="ExternalInput").ap())
    args.append(nc.dram_tensor("out", (B, S, D), F32, kind="ExternalOutput").ap())
    layer(nc, *args)
    return run_bass_kernel_spmd(nc, [arrays], core_ids=[0]).results[0]["out"]
```

```python
from contextlib import ExitStack

import concourse.bass as bass
from concourse import mybir

ACT = mybir.ActivationFunctionType
ALU = mybir.AluOpType
AX = mybir.AxisListType
F32 = mybir.dt.float32
BF16 = mybir.dt.bfloat16
I32 = mybir.dt.int32

P = 128
B = 2
S = 1024
D = 256
HD = 16
NEXP = 8
ROUNDS = 3
HG = 4
GROUPS = D // (HD * HG)
GW = HD * HG
BG = B * GROUPS
STEPS = ROUNDS * BG
TB = S // P
NT = B * TB
KS = 96
KM = 99
EPS = 1e-5
KEY_SCALE = HD ** -0.5
NEG = -10000.0
ROW_LOW = -3.0e38

NAT = []
for _i in range(TB):
    for _c in range(1 if _i < 4 else 2):
        _w = P * (_i + 1) if _i < 4 else (512 if _c == 0 else P * (_i - 3))
        _nh = 4 if _w == 128 else 2 if _w == 256 else 1
        for _h in range(0, HG, _nh):
            NAT.append((_i, _c, list(range(_h, _h + _nh)), 512 * _c, _w, _i < 4 or _c == 1))
NN = len(NAT)

QUADS = []
for _t in range(2):
    for _j in range(4 * (_t + 1)):
        _k = max(0, _j - 4 * _t)
        QUADS.append((_t, _j, 512 - P * _k, P * _k, _j >= 4 * _t))
NQ = len(QUADS)


def head_chunks(w):
    if w > 256:
        return [[0], [1], [2], [3]], 512
    return [[0, 1], [2, 3]], w


CHUNKS_TO = [0]
MASKS_TO = [0]
for _q in QUADS:
    CHUNKS_TO.append(CHUNKS_TO[-1] + len(head_chunks(_q[2])[0]))
    MASKS_TO.append(MASKS_TO[-1] + _q[4])
NC, NM = CHUNKS_TO[-1], MASKS_TO[-1]
RING3 = 3

ORDER = """
    A A
    B B A A B B V
    B A A B max1 V A B B A copy1
    B ctx0 A B A V ctx1
    B A A B V hi A
    B B V B A A rest B V copy0 A A
    B B A mid V A B A B A
    B A low parts0 B A B qt0 B
    B A A V B A A A B qt1 B A
    B A B V A B A max0 B A
    B V B B A A A B
    B B A V A
    B V B parts1
"""


def plan_step():
    plan, a, v = [], 0, -2
    chunks = iter([("st", qd, c) for qd in range(NQ) for c in range(len(head_chunks(QUADS[qd][2])[0]))])
    for word in ORDER.split():
        if word == "A":
            plan.append(("nat", a))
            a += 1
        elif word == "B":
            plan.append(next(chunks))
        elif word == "V":
            plan.append(("pv", v))
            v += 1
        elif word[-1].isdigit():
            plan.append((word[:-1], int(word[-1])))
        else:
            plan.append((word,))
    return plan


PLAN = plan_step()
NAT_HALF = sum(c[0] < 4 for c in NAT)


def plan_experts():
    order = [("turn", 2), ("turn", 3), ("mul", 2), ("turn", 4), ("mul", 3)]
    for e in range(5, NEXP):
        order += [("turn", e), ("mul", e - 1)]
    order.append(("mul", NEXP - 1))
    plan, c = [], 0
    for kind, e in order:
        for part in range(4):
            plan.append((kind, e, part))
            if order.index((kind, e)) >= 6:
                more = min(NN - c, 1 if kind == "turn" else 2)
                plan += [("nat", k) for k in range(c, c + more)]
                c += more
    plan += [("nat", k) for k in range(c, NN)]
    plan.insert(plan.index(("mul", NEXP - 1, 2)), ("max",))
    return plan


EXPERT_PLAN = plan_experts()

TAIL = [(kind, a) for kind in ("ctx", "out") for a in range(4)]
TAIL_AT = dict(zip((0, 2, 5, 8, 14, 19, 24, 29), range(len(TAIL))))
TAIL_FIRST = len(TAIL)
TAIL += [("norm", 0), ("norm", 1), ("ctx", 4), ("ctx", 5), ("norm", 2), ("norm", 3), ("ffn", 0), ("out", 4), ("out", 5),
         ("ctx", 6), ("ctx", 7), ("ffn", 1), ("out", 6), ("out", 7), ("ffn", 2), ("ffn", 3),
         ("norm", 4), ("norm", 5), ("ffn", 4), ("ffn", 5), ("norm", 6), ("norm", 7), ("ffn", 6), ("ffn", 7)]
TAIL_BANK = [3 + u % 3 if u < TAIL_FIRST else (3, 4, 5, 0, 1, 2)[(u - TAIL_FIRST) % 6] for u in range(len(TAIL))]
TAIL_BY_ACT = [u >= TAIL_FIRST and kind in ("ctx", "norm") for u, (kind, _) in enumerate(TAIL)]

PIECES_Q = (0, 1, 2, 0, 1, 0)
PIECES_K = (0, 0, 0, 1, 1, 2)
LOADS = len(PIECES_Q) + len(PIECES_K) + 1
CWRITES = 3
PROJ_WRITES = 48
WBASE = PROJ_WRITES // 3 * 16


def wait_alone(eng, sem, value, tally):
    eng.wait_ge(sem, value)
    eng.sem_inc(tally, 1)


class Step:

    def __init__(self, i, off):
        self.i, self.off = i, off
        self.n = 3 * i + off
        self.u = off % 3
        self.q = i + off // 3

    def bank(self, per_step, k):
        return (per_step * self.off + k) % RING3

    def add(self, d):
        return Step(self.i, self.off + d)


def over_steps(eng, step):
    step(Step(0, 0), has_ctx=False, has_split=False, has_next=True)
    turns = (STEPS - BG) // 3
    with eng.Fori(0, turns) as i:
        for k in range(3):
            step(Step(i, 1 + k), has_ctx=True, has_split=True, has_next=True)
    step(Step(turns, 1), has_ctx=True, has_split=True, has_next=True)
    with eng.Fori(turns, turns + 2) as i:
        for k in range(3):
            step(Step(i, 2 + k), has_ctx=True, has_split=False, has_next=True)
    step(Step(turns + 2, 2), has_ctx=True, has_split=False, has_next=False)


def layer(nc, x, tok_w, wqkv, bqkv, out_w, out_b, w1, w2, out):
    with ExitStack() as ctx:
        def sb(name, shape, dt):
            return ctx.enter_context(nc.sbuf_tensor(name, shape, dt))

        def sem(name):
            return ctx.enter_context(nc.semaphore(name))

        q_d = nc.dram_tensor("q_parts", [BG, 3, 2, GW, 512], BF16, kind="Internal").ap()
        k_d = nc.dram_tensor("k_parts", [BG, 3, GW, S], BF16, kind="Internal").ap()
        v_d = nc.dram_tensor("v_ones", [BG, P, TB, 2 * GW], F32, kind="Internal").ap()
        c_d = nc.dram_tensor("context", [BG, P, TB * GW], F32, kind="Internal").ap()

        ps = ctx.enter_context(nc.psum_tensor("ps", [P, 8, 512], F32))
        ST_BANK, NAT_BANK, PV_BANK, MISC_BANK = 0, 3, 6, 7
        W_BANK = (MISC_BANK, PV_BANK)
        misc = ps[:, MISC_BANK, :]
        misc_bf = misc.bitcast(BF16)

        h = sb("h", [P, NT, D], F32)
        xT = sb("xT", [P, 2, B * S], F32)
        wn = sb("wn", [P, 6, D], F32)
        wT = sb("wT", [P, 2, 3 * D], F32)
        own = sb("own", [P, 2, D], F32)
        owp = sb("owp", [P, 2, D], F32)
        woT = sb("woT", [P, 2, D], F32)
        bias_qk = sb("bias_qk", [P, 4], F32)
        bias_v = sb("bias_v", [P, D], F32)
        bias_o = sb("bias_o", [P, D], F32)
        idx_row = sb("idx_row", [NT, P], I32)
        idx_f = sb("idx_f", [NT, P], F32)
        idx = sb("idx", [P, NT], I32)
        bias_row = sb("bias_row", [4, P], F32)
        bias_p = sb("bias_p", [4, P], F32)
        identf = sb("identf", [P, P], F32)
        identb = sb("identb", [P, P], BF16)
        mask_l = sb("mask_l", [P, P], BF16)
        mask_r = sb("mask_r", [P, P], BF16)
        stats = sb("stats", [P, NT, 6], F32)
        mv = sb("mv", [P, NT, 2], F32)
        var = sb("var", [P, NT], F32)
        std = sb("std", [P, NT], F32)
        rstd = sb("rstd", [P, NT], F32)
        hn = sb("hn", [P, 4, D], F32)
        vt = sb("vt", [P, 4, GROUPS, HG, 2, HD], F32)
        w12 = sb("w12", [P, 2, D], F32)
        work = sb("work", [P, 12288], F32)
        qst = sb("qst", [P, 3, HG * S], BF16)
        kst = sb("kst", [P, 3, HG * S], BF16)
        vst = sb("vst", [P, 3, TB, HG, 2 * HD], F32)
        mx = sb("mx", [P, HG, TB, 2], F32)
        negm = sb("negm", [P, 2, HG * 4], F32)
        mrest = sb("mrest", [P, 2, HG * 4], F32)
        msp = sb("msp", [P, 2, 3, HG * 4], BF16)
        mrow = sb("mrow", [48, 2, P], BF16)
        cT = sb("cT", [P, 2, 512], F32)
        rden = sb("rden", [P, 16], F32)
        cn = sb("cn", [P, TB, HD, HG], F32)
        crest = sb("crest", [P, TB, GW], F32)
        qn = sb("qn", [P, TB, 3, GW], BF16)
        qT1 = sb("qT1", [P, S], BF16)
        qT2 = sb("qT2", [GW, S], BF16)

        w1b = work[:, 0:4096].rearrange("p (u k n) -> p u k n", u=2, k=2)
        w2b = work[:, 4096:8192].rearrange("p (u k n) -> p u k n", u=2, k=8)
        w1T = work[:, 8192:12288].rearrange("p (u k n) -> p u k n", u=2, k=8)
        prob = work[:, 0:6144].rearrange("p (s c) -> p s c", s=3)
        cx = work[:, 6144:10240].rearrange("p (k c) -> p k c", k=NT)
        hn2 = cx
        xs = qst[:, 0, 0:3072].bitcast(F32).rearrange("p (r n) -> p r n", r=3)
        rs = qst[:, 1, 0:3072].bitcast(F32).rearrange("p (r n) -> p r n", r=3)
        parts = [t[:, 2, 1536 * r:1536 * (r + 1)].rearrange("p (a n) -> p a n", a=3)
                 for t in (qst, kst) for r in range(2)]

        in_x, in_w, in_b = sem("in_x"), sem("in_w"), sem("in_b")
        consts, ones_set = sem("consts"), sem("ones_set")
        rows_ready, rows_turned, idx_ready = sem("rows_ready"), sem("rows_turned"), sem("idx_ready")
        gathered = [sem(f"gathered{n}") for n in range(4)]
        dchain = sem("dve_chain")
        pchain = sem("pool_chain")
        bias_ready, h_biased = sem("bias_ready"), sem("h_biased")
        var_ready, std_ready = sem("var_ready"), sem("std_ready")
        hn_ready = sem("hn_ready")
        owp_ready = sem("owp_ready")
        job_done, job_act, job_dve = sem("job_done"), sem("job_act"), sem("job_dve")
        x_hi, x_rest, x_mid, x_lo = sem("x_hi"), sem("x_rest"), sem("x_mid"), sem("x_lo")
        part_out = [sem(f"part_out{r}") for r in range(4)]
        vt_out = [sem(f"vt_out{r}") for r in range(4)]
        w_first = [sem(f"w_first{e}") for e in range(2)]
        w_second = [sem(f"w_second{e}") for e in range(2)]
        w1_loaded = [sem(f"w1_loaded{r}") for r in range(2)]
        w2_loaded = [sem(f"w2_loaded{r}") for r in range(2)]
        w_turned, w_evac = sem("w_turned"), sem("w_evac")
        w_mul, w_acc = sem("w_mul"), sem("w_acc")
        stack_in = [sem(f"stack_in{u}") for u in range(3)]
        max_in = [sem(f"max_in{T}") for T in range(2)]
        scratch = [sem(f"scratch{u}") for u in range(3)]
        nat_ready, nat_used = sem("nat_ready"), sem("nat_used")
        max_neg, max_split = sem("max_neg"), sem("max_split")
        max_turned, max_rows = sem("max_turned"), sem("max_rows")
        st_ready, exp_done, mask_done, prob_used = (sem("st_ready"), sem("exp_done"),
                                                    sem("mask_done"), sem("prob_used"))
        pv_copied = sem("pv_copied")
        ctx_turned, den_ready, ctx_ready = sem("ctx_turned"), sem("den_ready"), sem("ctx_ready")
        split_act, split_pool = sem("split_act"), sem("split_pool")
        q_turned, q_rows = sem("q_turned"), sem("q_rows")
        ctx_in = [sem(f"ctx_in{b}") for b in range(B)]
        ctx_last = [sem(f"ctx_last{T}") for T in range(2)]
        tail_done, tail_act, tail_dve = sem("tail_done"), sem("tail_act"), sem("tail_dve")
        e_var, e_std = sem("e_var"), sem("e_std")
        e_hn = sem("e_hn")
        pool_tally, pe_tally = sem("pool_tally"), sem("pe_tally")
        stored = sem("stored")

        jobs = [("wqkv", kc, half) for kc in range(2) for half in range(2)] + [("wo", 0, 0)]
        jobs += [("turn", 0, 0), ("turn", 1, 0)]
        for n in range(4):
            jobs += [("qk", m, n) for m in range(4)]
            if n < 3:
                jobs += [("turn", 2 * n + 2, 0), ("turn", 2 * n + 3, 0)]
            jobs += [("v", 2 * n, 0), ("v", 2 * n + 1, 0)]
        RING = 6

        def norm_ahead(kind, a, c):
            if kind == "turn" and a == 0:
                return 0
            return c + 1 if kind == "qk" and a == 0 and c < 3 else None

        by_dve = [j[0] == "v" for j in jobs]

        def copied(e, k):
            if by_dve[k]:
                e.wait_ge(job_dve, sum(by_dve[:k + 1]))
            else:
                e.wait_ge(job_act, k + 1 - sum(by_dve[:k + 1]))

        def tail_read(e, u):
            if TAIL_BY_ACT[u]:
                e.wait_ge(tail_act, sum(TAIL_BY_ACT[:u + 1]))
            else:
                e.wait_ge(tail_dve, u + 1 - sum(TAIL_BY_ACT[:u + 1]))

        block = ctx.enter_context(nc.Block())

        @block.sync
        def _(sp):
            sp.dma_start(idx_row[:], x.rearrange("b (k p) -> (b k) p", p=P)).then_inc(in_x, 16)
            sp.dma_start(bias_row[:], bqkv[0:2 * D].rearrange("(m p) -> m p", p=P)).then_inc(in_x, 16)
            for m in range(4):
                for g in range(2):
                    row = m * P + g * GW
                    sp.dma_start(wn[g * GW:(g + 1) * GW, m, :],
                                 wqkv[row:row + GW, :].rearrange("(h d) c -> d h c", h=HG)).then_inc(in_w, 16)
            sp.dma_start(wn[:, 4:6, :], wqkv[2 * D:3 * D, :].rearrange("(m p) c -> p m c", p=P)).then_inc(in_w, 16)
            sp.dma_start(own[:], out_w.rearrange("(m p) c -> p m c", p=P)).then_inc(in_w, 16)
            sp.dma_start(bias_v[:], bqkv[2 * D:3 * D].partition_broadcast(P)).then_inc(in_b, 16)
            sp.dma_start(bias_o[:], out_b.partition_broadcast(P)).then_inc(in_b, 16)

            for n in range(4):
                b, half = n // 2, n % 2
                for m in range(4):
                    x_n = 4 * n + m
                    sp.wait_ge(x_lo, x_n + 1)
                    for g in range(2):
                        at = GROUPS * b + 2 * (m % 2) + g
                        dst = q_d[at, :, half] if m < 2 else k_d[at, :, :, 512 * half:512 * half + 512]
                        sp.dma_start(dst.rearrange("a r t -> r a t"),
                                     parts[x_n % 4][g * GW:(g + 1) * GW]).then_inc(part_out[x_n % 4], 16)
                for k in range(4 * n, 4 * n + 4):
                    sp.wait_ge(job_dve, k // 2 + 1)
                    dst = v_d[GROUPS * b:GROUPS * (b + 1), :, k % TB, :].rearrange("g s f -> s g f")
                    sp.dma_start(dst, vt[:, k % 4].rearrange("p g h o d -> p g (h o d)")).then_inc(vt_out[k % 4], 16)
            for r in range(4):
                sp.wait_ge(part_out[r], 16 * 8)
                sp.wait_ge(vt_out[r], 16 * 4)

            def load(s):
                at = s.n % BG
                for k, (pq, pk) in enumerate(zip(PIECES_Q, PIECES_K)):
                    rows = slice(k * HD, (k + 1) * HD)
                    sp.dma_start(qst[rows, s.u, :].rearrange("p (T c) -> p T c", T=2), q_d[at, pq].rearrange("T (d h) t -> d T (h t)", h=HG)).then_inc(stack_in[s.u], 16)
                    sp.dma_start(kst[rows, s.u, :], k_d[at, pk].rearrange("(d h) t -> d (h t)", h=HG)).then_inc(stack_in[s.u], 16)
                sp.dma_start(vst[:, s.u].rearrange("p j h d -> p (j h d)"),
                             v_d[at].rearrange("s j f -> s (j f)")).then_inc(stack_in[s.u], 16)

            def max_to_stack(s, T):
                sp.wait_ge(max_rows, 2 * s.n + T + 1)
                for a in range(3):
                    dst = qst[KS + a:KS + a + 1, s.u, 2048 * T:2048 * (T + 1)].rearrange("p (r t) -> p r t", t=P)
                    sp.dma_start(dst, mrow[16 * a:16 * a + 16, T, :]).then_inc(max_in[T], 16)

            def context_out(s):
                sp.wait_ge(ctx_ready, 2 * s.n + 2)
                sp.dma_start(c_d[s.n % BG], cn[:].rearrange("p j d h -> p (j d h)")).then_inc(scratch[s.u], 16)
                sp.sem_inc(scratch[s.u], 16 * (CWRITES - 1))

            def load_contexts(steps, *counts):
                for u, count in enumerate(counts):
                    sp.wait_ge(scratch[u], WBASE + 16 * CWRITES * count)
                for at in steps:
                    b, g = at // GROUPS, at % GROUPS
                    sp.dma_start(cx[:, TB * b:TB * (b + 1), GW * g:GW * (g + 1)],
                                 c_d[at].rearrange("p (j c) -> p j c", j=TB)).then_inc(ctx_in[b], 16)

            def step(s, has_ctx, has_split, has_next, has_load=True):
                max_to_stack(s, 1)
                if not has_load and has_next:
                    load_contexts(range(GROUPS), 7, 7, 6)
                if has_load:
                    if has_ctx:
                        sp.wait_ge(prob_used, NQ * s.n)
                        sp.wait_ge(scratch[s.u], WBASE + 16 * CWRITES * (s.q - 1))
                    load(s.add(2))
                if has_ctx:
                    c = s.add(-1)
                    at = c.n % BG
                    if not has_split:
                        sp.wait_ge(scratch[c.u], WBASE + 16 * CWRITES * c.q)
                        context_out(c)
                if has_split:
                    sp.wait_ge(q_rows, 2 * c.n + 1)
                    for a in range(2):
                        sp.dma_start(q_d[at, a].rearrange("T r t -> r T t"),
                                     qT1[a * GW:(a + 1) * GW, :].rearrange("r (T t) -> r T t", T=2)).then_inc(scratch[c.u], 16)
                    sp.wait_ge(q_rows, 2 * c.n + 2)
                    sp.dma_start(q_d[at, 2].rearrange("T r t -> r T t"),
                                 qT2[:].rearrange("r (T t) -> r T t", T=2)).then_inc(scratch[c.u], 16)
                if has_next:
                    max_to_stack(s.add(1), 0)

            for u in range(3):
                sp.sem_inc(scratch[u], WBASE)
            load(Step(0, 0))
            load(Step(0, 1))
            max_to_stack(Step(0, 0), 0)
            step(Step(0, 0), has_ctx=False, has_split=False, has_next=True)
            turns = (STEPS - BG) // 3
            with sp.Fori(0, turns) as i:
                for k in range(3):
                    step(Step(i, 1 + k), has_ctx=True, has_split=True, has_next=True)
            for n in range(3 * turns + 1, STEPS):
                step(Step(n // 3, n % 3), has_ctx=True, has_split=n <= STEPS - BG, has_next=n < STEPS - 1,
                     has_load=n < STEPS - 2)

            load_contexts(range(GROUPS, BG - 1), 8, 8, 7)
            for T in range(2):
                sp.wait_ge(ctx_ready, 2 * STEPS - 1 + T)
                sp.dma_start(cx[:, NT - TB + 4 * T:NT - TB + 4 * T + 4, D - GW:D],
                             cn[:, 4 * T:4 * T + 4].rearrange("p j d h -> p j (d h)")).then_inc(ctx_last[T], 16)
            for a in range(NT // 2):
                tail_read(sp, TAIL.index(("ffn", a)))
                sp.dma_start(out.rearrange("b (j p) d -> p (b j) d", p=P)[:, 2 * a:2 * a + 2, :],
                             h[:, 2 * a:2 * a + 2, :]).then_inc(stored, 16)
            sp.wait_ge(stored, 16 * NT // 2)

        @block.gpsimd
        def _(pool):
            count = [0]

            def link(ins):
                count[0] += 1
                ins.then_inc(pchain, 1)
                pool.wait_ge(pchain, count[0])

            link(pool.memset(identf[:], 0.0))
            pool.affine_select(out=identf[:], in_=identf[:], compare_op=ALU.not_equal, fill=1.0,
                               base=0, pattern=[[-1, P]], channel_multiplier=1).then_inc(consts, 1)
            pool.wait_ge(consts, 1)
            pool.tensor_copy(identb[:], identf[:]).then_inc(consts, 1)
            link(pool.memset(mask_l[:], 0.0))
            pool.affine_select(out=mask_l[:], in_=mask_l[:], compare_op=ALU.not_equal, fill=125.0,
                               base=0, pattern=[[-1, P]], channel_multiplier=1).then_inc(consts, 1)
            link(pool.memset(mask_r[:], 0.0))
            pool.affine_select(out=mask_r[:], in_=mask_r[:], compare_op=ALU.is_ge, fill=NEG / 125.0,
                               base=0, pattern=[[-1, P]], channel_multiplier=1).then_inc(consts, 1)
            pool.memset(vt[:], 1.0).then_inc(consts, 1)
            pool.wait_ge(idx_ready, 1)
            for k in range(NT):
                pool.indirect_dma_start(
                    out=h[:, k, :], out_offset=None, in_=tok_w,
                    in_offset=bass.IndirectOffsetOnAxis(ap=idx[:, k:k + 1], axis=0)).then_inc(gathered[k // 4], 16)

            def load_w1(e):
                if e >= 4:
                    pool.wait_ge(w_turned, 4 * (e - 1))
                pool.dma_start(w1b[:, e % 2], w1[e].rearrange("(k p) n -> p k n", p=P)).then_inc(w1_loaded[e % 2], 16)

            def load_w2(e):
                if e >= 4:
                    pool.wait_ge(w_mul, e - 1)
                pool.dma_start(w2b[:, e % 2], w2[e].rearrange("(k p) n -> p k n", p=P)).then_inc(w2_loaded[e % 2], 16)

            pool.wait_ge(w_mul, 2)
            for e in range(2, 4):
                load_w1(e)
                load_w2(e)
            pool.wait_ge(consts, 5)
            for u in range(2):
                pool.memset(kst[KS:KM, u, :], 1.0).then_inc(ones_set, 1)
                pool.wait_ge(ones_set, u + 1)
            pool.wait_ge(hn_ready, 4)
            pool.wait_ge(in_b, 16 * 2)
            pool.tensor_tensor(h[:], h[:], bias_o[:].unsqueeze(1).broadcast_to([P, NT, D]),
                               ALU.add).then_inc(h_biased, 1)
            pool.wait_ge(h_biased, 1)
            for r in range(4):
                pool.wait_ge(part_out[r], 16 * 8)
            pool.memset(kst[KS:KM, 2, :], 1.0).then_inc(ones_set, 1)
            pool.wait_ge(ones_set, 3)
            load_w1(4)
            for e in range(5, NEXP):
                load_w1(e)
                load_w2(e - 1)
            load_w2(NEXP - 1)

            def split_max(s, T):
                done = 8 * s.n + 4 * T
                wait_alone(pool, max_neg, 2 * s.n + T + 1, pool_tally)
                if not (isinstance(s.n, int) and s.n == 0):
                    wait_alone(pool, max_turned, 2 * s.n + T - 1, pool_tally)
                pool.tensor_copy(msp[:, T, 0, :], negm[:, T]).then_inc(max_split, 1)
                wait_alone(pool, max_split, done + 1, pool_tally)
                pool.tensor_tensor(mrest[:, T], negm[:, T], msp[:, T, 0, :], ALU.subtract).then_inc(max_split, 1)
                wait_alone(pool, max_split, done + 2, pool_tally)
                pool.tensor_copy(msp[:, T, 1, :], mrest[:, T]).then_inc(max_split, 1)
                wait_alone(pool, max_split, done + 3, pool_tally)
                pool.tensor_tensor(msp[:, T, 2, :], mrest[:, T], msp[:, T, 1, :], ALU.subtract).then_inc(max_split, 1)

            def step(s, has_ctx, has_split, has_next):
                c = s.add(-1)
                for what, *at in PLAN:
                    if what == "parts" and has_next:
                        split_max(s.add(1), at[0])
                    if what == "st" and QUADS[at[0]][4] and at[1] == len(head_chunks(QUADS[at[0]][2])[0]) - 1:
                        qd = at[0]
                        pitch = head_chunks(QUADS[qd][2])[1]
                        wait_alone(pool, exp_done, NC * s.n + CHUNKS_TO[qd + 1], pool_tally)
                        v = prob[:, qd % 3, 0:HG * pitch].rearrange("p (h c) -> p h c", c=pitch)[:, :, 0:P]
                        pool.affine_select(out=v, in_=v, compare_op=ALU.is_ge, fill=0.0, base=0,
                                           pattern=[[0, HG], [1, P]], channel_multiplier=-1).then_inc(mask_done, 1)
                    if what == "rest" and has_split:
                        wait_alone(pool, split_act, 2 * c.n + 1, pool_tally)
                        pool.tensor_tensor(crest[:], cn[:].rearrange("p j d h -> p j (d h)"), qn[:, :, 0, :],
                                           ALU.subtract).then_inc(split_pool, 1)
                    if what == "low" and has_split:
                        wait_alone(pool, split_act, 2 * c.n + 2, pool_tally)
                        pool.tensor_tensor(qn[:, :, 2, :], crest[:], qn[:, :, 1, :], ALU.subtract).then_inc(split_pool, 1)

            split_max(Step(0, 0), 0)
            split_max(Step(0, 0), 1)
            over_steps(pool, step)

        @block.scalar
        def _(act):
            for e in range(2):
                act.dma_start(w1b[:, e], w1[e].rearrange("(k p) n -> p k n", p=P)).then_inc(w_first[e], 16)
                act.wait_ge(in_w, 16 * 10)
                act.dma_start(w2b[:, e], w2[e].rearrange("(k p) n -> p k n", p=P)).then_inc(w_second[e], 16)

            def w_copies(e, r):
                for k in range(4):
                    act.wait_ge(w_turned, 4 * e + k + 1)
                    act.copy(w1T[:, r, 2 * k:2 * k + 2, :].rearrange("p a n -> p (a n)"),
                             ps[:, (4 * e + k) % 3, :]).then_inc(w_evac, 1)

            def make_mid(x_n):
                act.wait_ge(x_rest, x_n + 1)
                act.copy(parts[x_n % 4][:, 1, :], rs[:, x_n % 3, :]).then_inc(x_mid, 1)

            act.wait_ge(bias_ready, 1)
            x_n = 0
            for k, (kind, a, c) in enumerate(jobs):
                if kind == "turn" and a == 0:
                    w_copies(0, 0)
                n = norm_ahead(kind, a, c)
                if n is not None:
                    act.wait_ge(var_ready, n + 1)
                    act.activation(std[:, 4 * n:4 * n + 4], var[:, 4 * n:4 * n + 4],
                                   ACT.Sqrt).then_inc(std_ready, 1)
                if kind == "turn" and a == 0:
                    w_copies(1, 1)
                if not by_dve[k]:
                    act.wait_ge(job_done, k + 1)
                    bank = ps[:, k % RING, :]
                    if kind == "qk":
                        if x_n >= 3:
                            act.wait_ge(x_rest, x_n - 2)
                        act.activation(xs[:, x_n % 3, :], bank, ACT.Identity, bias=bias_qk[:, a:a + 1],
                                       scale=1.0 if a < 2 else KEY_SCALE).then_inc(job_act, 1)
                    elif kind == "wqkv":
                        w = 512 if c == 0 else 256
                        act.copy(wT[:, a, 512 * c:512 * c + w], bank[:, 0:w]).then_inc(job_act, 1)
                    elif kind == "wo":
                        act.copy(woT[:].rearrange("p k n -> p (k n)"), bank).then_inc(job_act, 1)
                    else:
                        act.copy(xT[:, :, 256 * a:256 * a + 256],
                                 bank.rearrange("p (k n) -> p k n", k=2)).then_inc(job_act, 1)
                if kind == "qk":
                    copied(act, k)
                    if x_n >= 4:
                        act.wait_ge(part_out[x_n % 4], 32 * (x_n // 4))
                    act.copy(parts[x_n % 4][:, 0, :], xs[:, x_n % 3, :]).then_inc(x_hi, 1)
                    if a >= 1:
                        make_mid(x_n - 1)
                    x_n += 1
                if kind == "v" and a % 2 == 0:
                    make_mid(x_n - 1)

            for e in range(2, NEXP):
                w_copies(e, e % 2)

            def tail_roots(n, count):
                act.wait_ge(e_var, n + count)
                act.activation(std[:, 4 * n:4 * (n + count)], var[:, 4 * n:4 * (n + count)],
                               ACT.Sqrt).then_inc(e_std, count)

            def copy_context(s, T):
                act.wait_ge(prob_used, NQ * s.n + (4 if T == 0 else NQ))
                act.copy(cT[:, T, :], ps[:, PV_BANK, :]).then_inc(pv_copied, 1)

            def copy_max(s, T):
                act.wait_ge(max_turned, 2 * s.n + T + 1)
                if not (isinstance(s.n, int) and s.n == 0):
                    act.wait_ge(max_in[T], 48 * s.n)
                act.copy(mrow[:, T, :], misc_bf[0:48, 0:P]).then_inc(max_rows, 1)

            def exps(s, qd, ci):
                w = QUADS[qd][2]
                chunks, pitch = head_chunks(w)
                if ci == 0 and not (isinstance(s.n, int) and NQ * s.n + qd < 3):
                    act.wait_ge(prob_used, NQ * s.n + qd - 2)
                ch, n = CHUNKS_TO[qd] + ci, len(chunks[ci])
                act.wait_ge(st_ready, NC * s.n + ch + 1)
                src = ps[:, ST_BANK + s.bank(NC, ch), 0:n * w].rearrange("p (h c) -> p h c", c=w)
                first = chunks[ci][0] * pitch
                dst = prob[:, qd % 3, first:first + n * pitch].rearrange("p (h c) -> p h c", c=pitch)[:, :, 0:w]
                act.activation(dst, src, ACT.Exp).then_inc(exp_done, 1)

            def step(s, has_ctx, has_split, has_next):
                c = s.add(-1)
                for what, *at in PLAN:
                    if what == "st":
                        exps(s, *at)
                    if what == "copy" and (at[0] == 0 or has_ctx):
                        copy_context(s if at[0] == 0 else c, at[0])
                    if what == "hi" and has_split:
                        act.wait_ge(ctx_ready, 2 * c.n + 2)
                        act.copy(qn[:, :, 0, :], cn[:].rearrange("p j d h -> p j (d h)")).then_inc(split_act, 1)
                    if what == "mid" and has_split:
                        act.wait_ge(split_pool, 2 * c.n + 1)
                        act.copy(qn[:, :, 1, :], crest[:]).then_inc(split_act, 1)
                    if what == "qt" and has_split:
                        act.wait_ge(q_turned, 2 * s.n - 1 + at[0])
                        if at[0] == 0:
                            act.copy(qT1[:], misc_bf).then_inc(q_rows, 1)
                        else:
                            act.copy(qT2[:], misc_bf[0:GW, :]).then_inc(q_rows, 1)
                    if what == "max" and at[0] == 0 and has_next:
                        copy_max(s.add(1), 0)
                    if what == "max" and at[0] == 1:
                        copy_max(s, 1)

            copy_max(Step(0, 0), 0)
            over_steps(act, step)
            tail_roots(0, 2)
            copy_context(Step(0, STEPS - 1), 1)

            for u in range(TAIL_FIRST, len(TAIL)):
                kind, a = TAIL[u]
                if (kind, a) in (("ctx", 6), ("norm", 6)):
                    tail_roots(2 if kind == "ctx" else 3, 1)
                if TAIL_BY_ACT[u]:
                    act.wait_ge(tail_done, u + 1)
                    act.copy(xT[:, :, 256 * a:256 * a + 256],
                             ps[:, TAIL_BANK[u], :].rearrange("p (k n) -> p k n", k=2)).then_inc(tail_act, 1)

        @block.vector
        def _(dve):
            count = [0]

            def link(ins):
                count[0] += 1
                ins.then_inc(dchain, 1)
                dve.wait_ge(dchain, count[0])

            def norm_stats(n, ready):
                for k in range(4 * n, 4 * n + 4):
                    last = dve.bn_stats(stats[:, k, :], h[:, k, :])
                link(last)
                for k in range(4 * n, 4 * n + 4):
                    last = dve.bn_aggr(mv[:, k, :], stats[:, k, :])
                link(last)
                dve.tensor_scalar_add(var[:, 4 * n:4 * n + 4], mv[:, 4 * n:4 * n + 4, 1], EPS).then_inc(ready, 1)

            def normalise(n, root, dst):
                dve.wait_ge(root, n + 1)
                link(dve.reciprocal(rstd[:, 4 * n:4 * n + 4], std[:, 4 * n:4 * n + 4]))
                for k in range(4 * n, 4 * n + 4):
                    last = dve.tensor_scalar(dst[:, k % dst.shape[1], :], h[:, k, :], mv[:, k, 0:1], rstd[:, k:k + 1],
                                             ALU.subtract, ALU.mult)
                return last

            dve.wait_ge(in_x, 32)
            dve.tensor_copy(idx_f[:], idx_row[:]).then_inc(rows_ready, 1)
            dve.tensor_copy(bias_p[:].rearrange("m (g d h) -> m g d h", d=HD, h=HG),
                            bias_row[:].rearrange("m (g h d) -> m g d h", h=HG, d=HD)).then_inc(rows_ready, 1)
            dve.wait_ge(rows_turned, 1)
            dve.tensor_copy(idx[:], misc[:, 0:NT]).then_inc(idx_ready, 1)
            link(dve.tensor_copy(bias_qk[:, 0:2], misc[:, NT:NT + 2]))
            dve.tensor_scalar(bias_qk[:, 2:4], misc[:, NT + 2:NT + 4], KEY_SCALE, None, ALU.mult).then_inc(bias_ready, 1)
            link(dve.memset(w12[:], 0.0))
            link(dve.memset(mx[:], ROW_LOW))
            dve.wait_ge(in_w, 16 * 10)
            for o in range(2):
                last = dve.tensor_copy(owp[:, o, :].rearrange("p (g d h) -> p g d h", d=HD, h=HG),
                                       own[:, o, :].rearrange("p (g h d) -> p g d h", d=HD, h=HG))
            last.then_inc(owp_ready, 1)
            dve.wait_ge(in_b, 16 * 2)

            def make_rest(x_n):
                dve.wait_ge(x_hi, x_n + 1)
                if x_n >= 3:
                    dve.wait_ge(x_lo, x_n - 2)
                dve.tensor_tensor(rs[:, x_n % 3, :], xs[:, x_n % 3, :], parts[x_n % 4][:, 0, :],
                                  ALU.subtract).then_inc(x_rest, 1)

            def make_low(x_n):
                dve.wait_ge(x_mid, x_n + 1)
                dve.tensor_tensor(parts[x_n % 4][:, 2, :], rs[:, x_n % 3, :], parts[x_n % 4][:, 1, :],
                                  ALU.subtract).then_inc(x_lo, 1)

            def w_add(e, r, first=False):
                dve.wait_ge(w_mul, e + 1)
                if not first:
                    dve.wait_ge(w_acc, e)
                dve.tensor_tensor(w12[:], w12[:], ps[:, W_BANK[r], :].rearrange("p (m n) -> p m n", m=2), ALU.add).then_inc(w_acc, 1)

            x_n = 0
            for k, (kind, a, c) in enumerate(jobs):
                n = norm_ahead(kind, a, c)
                if n is not None:
                    dve.wait_ge(gathered[n], 64)
                    norm_stats(n, var_ready)
                    if n >= 1:
                        dve.wait_ge(job_done, jobs.index(("turn", 2 * n - 1, 0)) + 1)
                    normalise(n, std_ready, hn).then_inc(hn_ready, 1)
                if kind == "turn" and a == 0:
                    w_add(0, 0, first=True)
                    w_add(1, 1)
                if kind == "qk":
                    make_rest(x_n)
                    if a >= 1:
                        make_low(x_n - 1)
                    x_n += 1
                if kind == "v":
                    if a % 2 == 0:
                        make_low(x_n - 1)
                    dve.wait_ge(job_done, k + 1)
                    for r in range(2):
                        blk = 2 * a + r
                        if blk < 4:
                            dve.wait_ge(consts, 5)
                        else:
                            dve.wait_ge(vt_out[blk % 4], 16 * (blk // 4))
                        last = dve.tensor_tensor(
                            vt[:, blk % 4, :, :, 0, :],
                            ps[:, k % RING, 256 * r:256 * r + 256].rearrange("p (g h d) -> p g h d", g=GROUPS, h=HG),
                            bias_v[:].rearrange("p (g h d) -> p g h d", g=GROUPS, h=HG), ALU.add)
                    last.then_inc(job_dve, 1)
            def row_max(s, c):
                i, half, heads, k0, w, diag = NAT[c]
                dve.wait_ge(nat_ready, NN * s.n + c + 1)
                if c == 0 and not (isinstance(s.n, int) and s.n == 0):
                    dve.wait_ge(max_neg, 2 * s.n)
                src = ps[:, NAT_BANK + s.bank(NN, c), 0:w * len(heads)].rearrange("p (h c) -> p h c", c=w)
                dve.tensor_reduce(mx[:, heads[0]:heads[-1] + 1, i, half], src, AX.X, ALU.max).then_inc(nat_used, 1)

            def finish_max(s, T):
                dve.wait_ge(nat_used, NN * s.n + (NN if T else NAT_HALF))
                if not (isinstance(s.n, int) and s.n == 0):
                    dve.wait_ge(max_split, 8 * s.n + 4 * T - 4)
                dve.tensor_reduce(negm[:, T].rearrange("p (h i) -> p h i", h=HG), mx[:, :, 4 * T:4 * T + 4, :],
                                  AX.X, ALU.max, negate=True).then_inc(max_neg, 1)

            def divide(s, T):
                dve.wait_ge(ctx_turned, 2 * s.n + T + 1)
                tile = misc.rearrange("p (j h c) -> p j h c", j=4, h=HG)
                dve.reciprocal(rden[:].rearrange("p (j h) -> p j h", j=4), tile[:, :, :, HD]).then_inc(den_ready, 1)
                dve.wait_ge(den_ready, 2 * s.n + T + 1)
                if T == 0 and not (isinstance(s.n, int) and s.n == 0):
                    p = s.add(-1)
                    dve.wait_ge(scratch[p.u], WBASE + 16 * CWRITES * (p.q + 1))
                dve.tensor_tensor(
                    cn[:, 4 * T:4 * T + 4].rearrange("p j d h -> p j h d"), tile[:, :, :, 0:HD],
                    rden[:].rearrange("p (j h) -> p j h", j=4).unsqueeze(3).broadcast_to([P, 4, HG, HD]),
                    ALU.mult).then_inc(ctx_ready, 1)

            def tail_unit(u):
                kind, a = TAIL[u]
                if TAIL_BY_ACT[u]:
                    return
                bank = ps[:, TAIL_BANK[u], :].rearrange("p (k n) -> p k n", k=2)
                dve.wait_ge(tail_done, u + 1)
                if kind in ("ctx", "norm"):
                    dve.tensor_copy(xT[:, :, 256 * a:256 * a + 256], bank).then_inc(tail_dve, 1)
                    return
                dve.tensor_tensor(h[:, 2 * a:2 * a + 2, :], h[:, 2 * a:2 * a + 2, :], bank, ALU.add).then_inc(tail_dve, 1)
                if kind == "out":
                    tail_read(dve, u)
                    for k in range(2 * a, 2 * a + 2):
                        last = dve.bn_stats(stats[:, k, :], h[:, k, :])
                    link(last)
                    for k in range(2 * a, 2 * a + 2):
                        last = dve.bn_aggr(mv[:, k, :], stats[:, k, :])
                    link(last)
                    if a % 2 == 1:
                        n = a // 2
                        dve.tensor_scalar_add(var[:, 4 * n:4 * n + 4], mv[:, 4 * n:4 * n + 4, 1], EPS).then_inc(e_var, 1)

            def tail_norm(n):
                normalise(n, e_std, hn2).then_inc(e_hn, 1)

            def step(s, has_ctx, has_split, has_next):
                for what, *at in PLAN:
                    if what == "nat" and not has_next:
                        if at[0] == 0:
                            dve.wait_ge(h_biased, 1)
                        if at[0] in TAIL_AT:
                            tail_unit(TAIL_AT[at[0]])
                    if what == "nat" and has_next:
                        row_max(s.add(1), at[0])
                        if at[0] in (NAT_HALF - 1, NN - 1):
                            finish_max(s.add(1), at[0] // (NN - 1))
                    if what == "ctx" and has_ctx:
                        divide(s.add(-1), at[0])

            for what, at, *part in [u for u in EXPERT_PLAN if u[0] != "max"]:
                if what == "nat":
                    row_max(Step(0, 0), at)
                    if at in (NAT_HALF - 1, NN - 1):
                        finish_max(Step(0, 0), at // (NN - 1))
                if what == "mul" and part[0] == 3:
                    w_add(at, at % 2)
            over_steps(dve, step)
            divide(Step(0, STEPS - 1), 0)
            tail_norm(0)
            divide(Step(0, STEPS - 1), 1)
            tail_norm(1)
            for u in range(TAIL_FIRST, len(TAIL)):
                tail_unit(u)
                if TAIL[u] in (("out", 5), ("out", 7)):
                    tail_norm(TAIL[u][1] // 2)

        @block.tensor
        def _(pe):
            pe.wait_ge(consts, 1)
            pe.wait_ge(rows_ready, 2)
            pe.transpose(misc[:, 0:NT], idx_f[:], identf[0:NT, 0:NT])
            pe.transpose(misc[:, NT:NT + 4], bias_p[:], identf[0:4, 0:4]).then_inc(rows_turned, 1)
            def turn_w(e, part):
                r = e % 2
                if part == 0:
                    if e < 2:
                        pe.wait_ge(w_first[r], 16)
                    else:
                        pe.wait_ge(w1_loaded[r], 16 * (e // 2))
                if 4 * e + part >= 3:
                    pe.wait_ge(w_evac, 4 * e + part - 2)
                for k in range(2 * part, 2 * part + 2):
                    for kc in range(2):
                        at = 256 * (k % 2) + P * kc
                        last = pe.transpose(ps[:, (4 * e + part) % 3, at:at + P],
                                            w1b[:, r, kc, P * k:P * (k + 1)], identf[:])
                last.then_inc(w_turned, 1)

            def mul_w(e, part):
                r, m, half = e % 2, part // 2, part % 2
                if part == 0:
                    pe.wait_ge(w_evac, 4 * e + 4)
                    if e < 2:
                        pe.wait_ge(w_second[r], 16)
                    else:
                        pe.wait_ge(w2_loaded[r], 16 * (e // 2))
                        pe.wait_ge(w_acc, e - 1)
                for k in range(4 * half, 4 * half + 4):
                    last = pe.matmul(ps[:, W_BANK[r], m * D:(m + 1) * D], w1T[:, r, k, m * P:(m + 1) * P],
                                     w2b[:, r, k, :], start=(k == 0), stop=(k == 7))
                if part == 3:
                    last.then_inc(w_mul, 1)

            for k, (kind, a, c) in enumerate(jobs):
                if kind == "turn" and a == 0:
                    for j in range(k):
                        copied(pe, j)
                    for e in range(2):
                        for part in range(4):
                            turn_w(e, part)
                    pe.wait_ge(bias_ready, 1)
                    for e in range(2):
                        for part in range(4):
                            mul_w(e, part)
                    pe.wait_ge(w_evac, 8)
                if k >= RING:
                    copied(pe, k - RING)
                bank = ps[:, k % RING, :]
                if kind == "wqkv":
                    pe.wait_ge(in_w, 16 * 10)
                    for x_m, m in enumerate(range(4 * c, 4 * c + (4 if c == 0 else 2))):
                        last = pe.transpose(bank[:, x_m * P:(x_m + 1) * P], wn[:, m, a * P:(a + 1) * P], identf[:])
                elif kind == "wo":
                    pe.wait_ge(owp_ready, 1)
                    for kc in range(2):
                        for o in range(2):
                            last = pe.transpose(bank[:, (2 * kc + o) * P:(2 * kc + o + 1) * P],
                                                owp[:, o, kc * P:(kc + 1) * P], identf[:])
                elif kind == "turn":
                    pe.wait_ge(hn_ready, a // 2 + 1)
                    for kc in range(2):
                        for r in range(2):
                            last = pe.transpose(bank[:, 256 * kc + P * r:256 * kc + P * (r + 1)],
                                                hn[:, (2 * a + r) % 4, kc * P:(kc + 1) * P], identf[:])
                elif kind == "qk":
                    copied(pe, max(j for j in range(k) if jobs[j][0] == "turn" and jobs[j][1] <= 2 * c + 1))
                    for kc in range(2):
                        last = pe.matmul(bank, wT[:, kc, a * P:(a + 1) * P], xT[:, kc, 512 * c:512 * c + 512],
                                         start=(kc == 0), stop=(kc == 1))
                else:
                    for r in range(2):
                        blk = 2 * a + r
                        for kc in range(2):
                            last = pe.matmul(bank[:, 256 * r:256 * r + 256], xT[:, kc, blk * P:(blk + 1) * P],
                                             wT[:, kc, 2 * D:3 * D], start=(kc == 0), stop=(kc == 1))
                last.then_inc(job_done, 1)

            for k in range(len(jobs) - RING, len(jobs)):
                copied(pe, k)

            def row_scores(s, c):
                i, half, heads, k0, w, diag = NAT[c]
                if not (isinstance(s.n, int) and NN * s.n + c < 3):
                    pe.wait_ge(nat_used, NN * s.n + c - 2)
                for x_h, a in enumerate(heads):
                    q0 = 2048 * (i // 4) + 512 * a + P * (i % 4)
                    o = ps[:, NAT_BANK + s.bank(NN, c), x_h * w:(x_h + 1) * w]
                    last = pe.matmul(o, qst[0:KS, s.u, q0:q0 + P],
                                     kst[0:KS, s.u, S * a + k0:S * a + k0 + w], start=True, stop=not diag)
                    if diag:
                        last = pe.matmul(o[:, w - P:w], mask_l[:], mask_r[:], start=False, stop=True)
                last.then_inc(nat_ready, 1)

            def key_scores(s, qd, ci):
                T, j, w, off, diag = QUADS[qd]
                chunks, pitch = head_chunks(w)
                ch = CHUNKS_TO[qd] + ci
                if j == 0 and ci == 0:
                    pe.wait_ge(max_in[T], 48 * (s.n + 1))
                if not (isinstance(s.n, int) and NC * s.n + ch < 3):
                    pe.wait_ge(exp_done, NC * s.n + ch - 2)
                for x_h, a in enumerate(chunks[ci]):
                    t0 = 2048 * T + 512 * a + off
                    last = pe.matmul(ps[:, ST_BANK + s.bank(NC, ch), x_h * w:(x_h + 1) * w],
                                     kst[0:KM, s.u, S * a + P * j:S * a + P * (j + 1)],
                                     qst[0:KM, s.u, t0:t0 + w], start=True, stop=True)
                last.then_inc(st_ready, 1)

            def values(s, qd):
                T, j, w, off, diag = QUADS[qd]
                pitch = head_chunks(w)[1]
                pe.wait_ge(exp_done, NC * s.n + CHUNKS_TO[qd + 1])
                if diag:
                    pe.wait_ge(mask_done, NM * s.n + MASKS_TO[qd + 1])
                if j == 0 and not (isinstance(s.n, int) and 2 * s.n + T == 0):
                    pe.wait_ge(pv_copied, 2 * s.n + T)
                for a in range(HG):
                    last = pe.matmul(ps[32 * a:32 * a + 32, PV_BANK, off:off + w], vst[:, s.u, j, a, :],
                                     prob[:, qd % 3, a * pitch:a * pitch + w], start=(j == 0), stop=(j == 4 * T + 3))
                last.then_inc(prob_used, 1)

            def turn_max(s, T):
                wait_alone(pe, max_split, 8 * s.n + 4 * T + 4, pe_tally)
                pe.transpose(misc_bf[0:48, 0:P], msp[:, T].rearrange("p a r -> p (a r)"), identb[:]).then_inc(max_turned, 1)

            def turn_context(s, T):
                pe.wait_ge(pv_copied, 2 * s.n + T + 1)
                if T == 0 and isinstance(s.n, int) and s.n == STEPS - 1:
                    pe.wait_ge(ctx_ready, 2 * s.n)
                elif T == 0:
                    pe.wait_ge(max_rows, 2 * s.n + 4)
                else:
                    pe.wait_ge(ctx_ready, 2 * s.n + 1)
                for j in range(4):
                    last = pe.transpose(misc[:, P * j:P * (j + 1)], cT[:, T, P * j:P * (j + 1)], identf[:])
                last.then_inc(ctx_turned, 1)

            def turn_queries(s, half):
                if half == 0:
                    pe.wait_ge(split_pool, 2 * s.n + 2)
                else:
                    wait_alone(pe, q_rows, 2 * s.n + 1, pe_tally)
                cols = slice(0, P) if half == 0 else slice(P, P + GW)
                rows = P if half == 0 else GW
                for j in range(TB):
                    last = pe.transpose(misc_bf[0:rows, P * j:P * (j + 1)],
                                        qn[:, j].rearrange("p a r -> p (a r)")[:, cols], identb[:])
                last.then_inc(q_turned, 1)

            def tail_unit(u):
                kind, a = TAIL[u]
                bank = ps[:, TAIL_BANK[u], :]
                before = [v for v in range(u) if TAIL_BANK[v] == TAIL_BANK[u]]
                if before:
                    tail_read(pe, before[-1])
                elif u < TAIL_FIRST:
                    pe.wait_ge(nat_used, NN * STEPS)
                if kind in ("ctx", "norm"):
                    if kind == "norm":
                        pe.wait_ge(e_hn, a // 2 + 1)
                    elif a < 4:
                        pe.wait_ge(ctx_in[0], 16 * GROUPS)
                    else:
                        pe.wait_ge(ctx_in[1], 16 * (GROUPS - 1))
                        pe.wait_ge(ctx_last[(a - 4) // 2], 16)
                    src = cx if kind == "ctx" else hn2
                    for kc in range(2):
                        for r in range(2):
                            last = pe.transpose(bank[:, 256 * kc + P * r:256 * kc + P * (r + 1)],
                                                src[:, 2 * a + r, kc * P:(kc + 1) * P], identf[:])
                else:
                    tail_read(pe, TAIL.index(("ctx" if kind == "out" else "norm", a)))
                    w = woT if kind == "out" else w12
                    for r in range(2):
                        k = 2 * a + r
                        for kc in range(2):
                            last = pe.matmul(bank[:, D * r:D * (r + 1)], xT[:, kc, k * P:(k + 1) * P], w[:, kc, :],
                                             start=(kc == 0), stop=(kc == 1))
                last.then_inc(tail_done, 1)

            def step(s, has_ctx, has_split, has_next):
                nxt, c = s.add(1), s.add(-1)
                for what, *at in PLAN:
                    if what == "nat" and not has_next and at[0] in TAIL_AT:
                        tail_unit(TAIL_AT[at[0]])
                    if what == "nat" and has_next:
                        if at[0] == 0:
                            pe.wait_ge(stack_in[nxt.u], 16 * LOADS * (nxt.q + 1))
                        row_scores(nxt, at[0])
                    if what == "st":
                        key_scores(s, *at)
                    if what == "pv" and (at[0] >= 0 or has_ctx):
                        values(*((s, at[0]) if at[0] >= 0 else (c, NQ + at[0])))
                    if what == "ctx" and has_ctx:
                        turn_context(c, at[0])
                    if what == "qt" and has_split:
                        turn_queries(c, at[0])
                    if what == "max" and at[0] == 0 and has_next:
                        if has_split:
                            pe.wait_ge(q_rows, 2 * s.n)
                        elif has_ctx:
                            pe.wait_ge(ctx_ready, 2 * s.n)
                        else:
                            pe.wait_ge(max_rows, 2)
                        turn_max(nxt, 0)
                    if what == "max" and at[0] == 1:
                        pe.wait_ge(max_rows, 2 * s.n + 1)
                        turn_max(s, 1)

            pe.wait_ge(consts, 5)
            for what, *at in EXPERT_PLAN:
                if what == "turn":
                    turn_w(*at)
                if what == "mul":
                    mul_w(*at)
                if what == "nat":
                    if at[0] == 0:
                        pe.wait_ge(stack_in[0], 16 * LOADS)
                    row_scores(Step(0, 0), at[0])
                if what == "max":
                    pe.wait_ge(w_acc, NEXP - 1)
                    turn_max(Step(0, 0), 0)
            pe.wait_ge(ones_set, 3)
            pe.wait_ge(w_evac, 4 * NEXP)
            pe.wait_ge(w_acc, NEXP)
            over_steps(pe, step)
            last_step = Step(0, STEPS - 1)
            turn_context(last_step, 0)
            values(last_step, NQ - 2)
            values(last_step, NQ - 1)
            turn_context(last_step, 1)
            for u in range(TAIL_FIRST, len(TAIL)):
                tail_unit(u)


def kernel(**inputs):
    import numpy as np
    import concourse.bacc as bacc
    from concourse.bass_utils import run_bass_kernel_spmd

    nc = bacc.Bacc("TRN2", target_bir_lowering=False, num_devices=1)
    names = ["x", "L0_tok_W", "L0_attn_Wqkv_w", "L0_attn_Wqkv_b", "L0_attn_out_w", "L0_attn_out_b",
             "L0_ffn_w1", "L0_ffn_w2"]
    arrays, args = {}, []
    for name in names:
        a = np.ascontiguousarray(inputs[name])
        arrays[f"in_{name}"] = a
        args.append(nc.dram_tensor(f"in_{name}", a.shape, mybir.dt.from_np(a.dtype), kind="ExternalInput").ap())
    args.append(nc.dram_tensor("out", (B, S, D), F32, kind="ExternalOutput").ap())
    layer(nc, *args)
    return run_bass_kernel_spmd(nc, [arrays], core_ids=[0]).results[0]["out"]
```
